# Optimizing a Trainium2 kernel written in Bass

```python
import numpy as np
import jax
import jax.numpy as jnp

def _softmax(x, axis=-1):
    return jax.nn.softmax(x, axis=axis)

def _gelu(x):
    return jax.nn.gelu(x, approximate=True)

def _silu(x):
    return jax.nn.silu(x)

def _sigmoid(x):
    return jax.nn.sigmoid(x)

def _layernorm(x, axis=-1, eps=1e-05):
    m = jnp.mean(x, axis=axis, keepdims=True)
    v = jnp.var(x, axis=axis, keepdims=True)
    return (x - m) / jnp.sqrt(v + eps)

def _scatter_add(tgt, idx, src, axis=0):
    return tgt.at[idx].add(src)

def _segment_sum(src, seg, n):
    return jax.ops.segment_sum(src, seg, n)
kernel_name = 'mk_cond_resid_d4_seqx_r8_7f607d'

def setup_inputs(seed: int=0):
    np.random.seed(seed)
    _w = jnp.asarray

    def _rec_inputs():
        import jax
        import jax.numpy as jnp
        _rk = jax.random.key(seed)
        x = -0.0003929 + 0.9999 * jax.random.normal(jax.random.fold_in(_rk, 1), (128, 32, 128), jnp.float32)
        _lenS = 32 - jax.random.randint(jax.random.fold_in(_rk, 7), (128,), 0, max(1, 32 // 4) + 1, jnp.int32)
        _lenS2 = 32 - jax.random.randint(jax.random.fold_in(_rk, 8), (128,), 0, max(1, 32 // 4) + 1, jnp.int32)
        itok_B_0_2 = jax.random.randint(jax.random.fold_in(_rk, 11), (128,), 0, 3, jnp.int32)
        itok_Sx32_0_1023 = jax.random.randint(jax.random.fold_in(_rk, 13), (32, 32), 0, 128, jnp.int32)
        condB_uprev = -0.456674 + 0.753242 * jax.random.normal(jax.random.fold_in(_rk, 15), (128,), jnp.float32)
        itok_B_0_7 = jax.random.randint(jax.random.fold_in(_rk, 16), (128,), 0, 8, jnp.int32)
        itok_B_0_15 = jax.random.randint(jax.random.fold_in(_rk, 17), (128,), 0, 16, jnp.int32)
        _validS = jnp.arange(32)[None, :] < _lenS[:, None]
        _validS2 = jnp.arange(32)[None, :] < _lenS2[:, None]
        _causal = jnp.tril(jnp.ones((32, 32), dtype=bool))
        mask_SxS_bk0 = jnp.logical_not(jnp.broadcast_to(_validS[0:1, :], (32, 32)))
        mask_Sx32_bk1 = jnp.ones((32, 32), dtype=bool)
        return (x, itok_B_0_2, itok_Sx32_0_1023, condB_uprev, itok_B_0_7, itok_B_0_15, mask_SxS_bk0, mask_Sx32_bk1)
    x, itok_B_0_2, itok_Sx32_0_1023, condB_uprev, itok_B_0_7, itok_B_0_15, mask_SxS_bk0, mask_Sx32_bk1 = _rec_inputs()

    def _L0_cond_setup():
        import jax, jax.numpy as jnp
        import numpy as np
        NEG_INF = -1e+30
        key = jax.random.key(seed)
        k1, k2, k3, k4, k5 = jax.random.split(key, 5)
        B, S, D, A = (16, 128, 128, 32)
        hidden = jax.random.normal(k1, (B, S, D), dtype=jnp.float32)
        W1 = jax.random.normal(k2, (D, A), dtype=jnp.float32) / np.sqrt(D)
        b1 = jax.random.normal(k3, (A,), dtype=jnp.float32) * 0.01
        v = jax.random.normal(k4, (A,), dtype=jnp.float32) / np.sqrt(A)
        prompt_type_ids = jax.random.randint(k5, (B,), 0, 3, dtype=jnp.int32)
        return {'hidden': hidden, 'W1': W1, 'b1': b1, 'v': v, 'prompt_type_ids': prompt_type_ids}
    _L0_cond_all = _L0_cond_setup()
    _L0_cond_in = {k: v for k, v in _L0_cond_all.items() if k in ('W1', 'b1', 'v')}
    del _L0_cond_all

    def _L1_cond_setup():
        import jax, jax.numpy as jnp
        import numpy as np
        B, S, D, H = (4, 128, 128, 16)
        DH = D // H
        K_SPARSE = 32
        LAMBDA_MAX, ALPHA = (10.0, 5.0)
        SPARSE_THRESHOLD = 1.0
        key = jax.random.key(seed)
        ks = jax.random.split(key, 12)
        x = jax.random.normal(ks[0], (B, S, D), dtype=jnp.float32)
        prior_mask = jax.random.bernoulli(ks[1], 0.1, (S, S))
        prior_indices = jax.random.randint(ks[2], (S, K_SPARSE), 0, S)
        prior_index_mask = jax.random.bernoulli(ks[3], 0.9, (S, K_SPARSE))
        prior_index_mask = prior_index_mask.at[:, 0].set(True)
        u_prev = jax.random.normal(ks[4], (B, 1), dtype=jnp.float32)
        sc = 1.0 / np.sqrt(D)
        Wq = jax.random.normal(ks[5], (D, D), dtype=jnp.float32) * sc
        Wk = jax.random.normal(ks[6], (D, D), dtype=jnp.float32) * sc
        Wv = jax.random.normal(ks[7], (D, D), dtype=jnp.float32) * sc
        Wo = jax.random.normal(ks[8], (D, D), dtype=jnp.float32) * sc
        bq = jnp.zeros((D,), jnp.float32)
        bk = jnp.zeros((D,), jnp.float32)
        bv = jnp.zeros((D,), jnp.float32)
        bo = jnp.zeros((D,), jnp.float32)
        return {'x': x, 'prior_mask': prior_mask, 'prior_indices': prior_indices, 'prior_index_mask': prior_index_mask, 'u_prev': u_prev, 'Wq': Wq, 'bq': bq, 'Wk': Wk, 'bk': bk, 'Wv': Wv, 'bv': bv, 'Wo': Wo, 'bo': bo}
    _L1_cond_all = _L1_cond_setup()
    _L1_cond_in = {k: v for k, v in _L1_cond_all.items() if k in ('Wq', 'bq', 'Wk', 'bk', 'Wv', 'bv', 'Wo', 'bo')}
    del _L1_cond_all

    def _L2_cond_setup():
        import jax, jax.numpy as jnp
        import numpy as np
        B, S, D, F = (32, 64, 128, 512)
        R_COMMON, R_DOMAIN, E = (16, 16, 8)
        ALPHA = 2.0

        def _expert_lora(x, expert_ids, Wa, Wb):
            Ab = Wa[expert_ids]
            Bb = Wb[expert_ids]
            low = jnp.einsum('bsd,brd->bsr', x, Ab)
            return ALPHA * jnp.einsum('bsr,bor->bso', low, Bb)
        key = jax.random.key(seed)
        ks = jax.random.split(key, 12)
        sd = lambda k, shape: jax.random.normal(k, shape, dtype=jnp.float32) * (1.0 / np.sqrt(shape[-1]))
        return {'hidden_states': jax.random.normal(ks[0], (B, S, D), dtype=jnp.float32), 'expert_ids': jax.random.randint(ks[1], (B,), 0, E, dtype=jnp.int32), 'wi': sd(ks[2], (F, D)), 'wo': sd(ks[3], (D, F)), 'common_wi_a': sd(ks[4], (R_COMMON, D)), 'common_wi_b': sd(ks[5], (F, R_COMMON)), 'common_wo_a': sd(ks[6], (R_COMMON, F)), 'common_wo_b': sd(ks[7], (D, R_COMMON)), 'experts_wi_a': sd(ks[8], (E, R_DOMAIN, D)), 'experts_wi_b': sd(ks[9], (F, R_DOMAIN)) * jnp.ones((E, 1, 1)) * 0.0 + sd(ks[9], (E, F, R_DOMAIN)), 'experts_wo_a': sd(ks[10], (E, R_DOMAIN, F)), 'experts_wo_b': sd(ks[11], (E, D, R_DOMAIN))}
    _L2_cond_all = _L2_cond_setup()
    _L2_cond_in = {k: v for k, v in _L2_cond_all.items() if k in ('wi', 'wo', 'common_wi_a', 'common_wi_b', 'common_wo_a', 'common_wo_b', 'experts_wi_a', 'experts_wi_b', 'experts_wo_a', 'experts_wo_b')}
    del _L2_cond_all

    def _L3_cond_setup():
        import jax, jax.numpy as jnp
        import numpy as np
        B, N, DIM = (32, 128, 128)
        HID = 512
        PART = 32
        OUT = 128
        SHARED = OUT - PART
        E = 16
        key = jax.random.key(seed)
        ks = jax.random.split(key, 8)
        s = 0.02
        return {'x': jax.random.normal(ks[0], (B, N, DIM), dtype=jnp.float32), 'indices': jax.random.randint(ks[1], (B,), 0, E, dtype=jnp.int64), 'fc1_w': jax.random.normal(ks[2], (HID, DIM), dtype=jnp.float32) * s, 'fc1_b': jnp.zeros((HID,), dtype=jnp.float32), 'fc2_w': jax.random.normal(ks[3], (SHARED, HID), dtype=jnp.float32) * s, 'fc2_b': jnp.zeros((SHARED,), dtype=jnp.float32), 'experts_w': jax.random.normal(ks[4], (E, PART, HID), dtype=jnp.float32) * s, 'experts_b': jnp.zeros((E, PART), dtype=jnp.float32)}
    _L3_cond_all = _L3_cond_setup()
    _L3_cond_in = {k: v for k, v in _L3_cond_all.items() if k in ('fc1_w', 'fc1_b', 'fc2_w', 'fc2_b', 'experts_w', 'experts_b')}
    del _L3_cond_all
    return {'x': x, 'itok_B_0_2': itok_B_0_2, 'itok_Sx32_0_1023': itok_Sx32_0_1023, 'condB_uprev': condB_uprev, 'itok_B_0_7': itok_B_0_7, 'itok_B_0_15': itok_B_0_15, 'mask_SxS_bk0': mask_SxS_bk0, 'mask_Sx32_bk1': mask_Sx32_bk1, 'L0_cond_W1': _L0_cond_in['W1'], 'L0_cond_b1': _L0_cond_in['b1'], 'L0_cond_v': _L0_cond_in['v'], 'L1_cond_Wq': _L1_cond_in['Wq'], 'L1_cond_bq': _L1_cond_in['bq'], 'L1_cond_Wk': _L1_cond_in['Wk'], 'L1_cond_bk': _L1_cond_in['bk'], 'L1_cond_Wv': _L1_cond_in['Wv'], 'L1_cond_bv': _L1_cond_in['bv'], 'L1_cond_Wo': _L1_cond_in['Wo'], 'L1_cond_bo': _L1_cond_in['bo'], 'L2_cond_wi': _L2_cond_in['wi'], 'L2_cond_wo': _L2_cond_in['wo'], 'L2_cond_common_wi_a': _L2_cond_in['common_wi_a'], 'L2_cond_common_wi_b': _L2_cond_in['common_wi_b'], 'L2_cond_common_wo_a': _L2_cond_in['common_wo_a'], 'L2_cond_common_wo_b': _L2_cond_in['common_wo_b'], 'L2_cond_experts_wi_a': _L2_cond_in['experts_wi_a'], 'L2_cond_experts_wi_b': _L2_cond_in['experts_wi_b'], 'L2_cond_experts_wo_a': _L2_cond_in['experts_wo_a'], 'L2_cond_experts_wo_b': _L2_cond_in['experts_wo_b'], 'L3_cond_fc1_w': _L3_cond_in['fc1_w'], 'L3_cond_fc1_b': _L3_cond_in['fc1_b'], 'L3_cond_fc2_w': _L3_cond_in['fc2_w'], 'L3_cond_fc2_b': _L3_cond_in['fc2_b'], 'L3_cond_experts_w': _L3_cond_in['experts_w'], 'L3_cond_experts_b': _L3_cond_in['experts_b']}

def reference(x, itok_B_0_2, itok_Sx32_0_1023, condB_uprev, itok_B_0_7, itok_B_0_15, mask_SxS_bk0, mask_Sx32_bk1, L0_cond_W1, L0_cond_b1, L0_cond_v, L1_cond_Wq, L1_cond_bq, L1_cond_Wk, L1_cond_bk, L1_cond_Wv, L1_cond_bv, L1_cond_Wo, L1_cond_bo, L2_cond_wi, L2_cond_wo, L2_cond_common_wi_a, L2_cond_common_wi_b, L2_cond_common_wo_a, L2_cond_common_wo_b, L2_cond_experts_wi_a, L2_cond_experts_wi_b, L2_cond_experts_wo_a, L2_cond_experts_wo_b, L3_cond_fc1_w, L3_cond_fc1_b, L3_cond_fc2_w, L3_cond_fc2_b, L3_cond_experts_w, L3_cond_experts_b):
    import jax
    import jax.numpy as jnp

    def _L0_cond_ref(hidden, W1, b1, v, prompt_type_ids):
        import jax, jax.numpy as jnp
        import numpy as np
        NEG_INF = -1e+30
        B, S, D = hidden.shape
        attn_in = jnp.tanh(jnp.einsum('bsd,da->bsa', hidden, W1) + b1)
        scores = jnp.einsum('bsa,a->bs', attn_in, v)
        idx = jnp.arange(S)
        j = idx[:, None]
        l = idx[None, :]
        prefix_m = l <= j
        postfix_m = l >= j
        cloze_m = l != j
        pt = prompt_type_ids[:, None, None]
        mask = jnp.where(pt == 0, prefix_m[None], jnp.where(pt == 1, postfix_m[None], cloze_m[None]))
        masked_scores = jnp.where(mask, scores[:, None, :], NEG_INF)
        p = jax.nn.softmax(masked_scores, axis=-1)
        cnt = jnp.sum(mask, axis=-1).astype(hidden.dtype)
        pooled = jnp.einsum('bjl,bld->bjd', p, hidden) / cnt[..., None]
        return pooled

    def _L1_cond_ref(x, prior_mask, prior_indices, prior_index_mask, u_prev, Wq, bq, Wk, bk, Wv, bv, Wo, bo):
        import jax, jax.numpy as jnp
        import numpy as np
        B, S, D, H = (4, 128, 128, 16)
        DH = D // H
        K_SPARSE = 32
        LAMBDA_MAX, ALPHA = (10.0, 5.0)
        SPARSE_THRESHOLD = 1.0
        Bb, Ss, Dd = x.shape
        scale = 1.0 / jnp.sqrt(jnp.asarray(DH, x.dtype))

        def proj(W, b):
            return (x @ W.T + b).reshape(Bb, Ss, H, DH).transpose(0, 2, 1, 3)
        Q, K, V = (proj(Wq, bq), proj(Wk, bk), proj(Wv, bv))
        lam = LAMBDA_MAX * jnp.exp(-ALPHA * u_prev.reshape(Bb))
        use_sparse = lam >= SPARSE_THRESHOLD
        scores = jnp.einsum('bhqd,bhkd->bhqk', Q, K) * scale
        prior_bias = jnp.where(prior_mask[:Ss, :Ss], 0.0, -1.0).astype(x.dtype)
        bias = lam[:, None, None, None] * prior_bias[None, None]
        dense_out = jnp.einsum('bhqk,bhkd->bhqd', jax.nn.softmax(scores + bias, axis=-1), V)
        idx = prior_indices[:Ss]
        Kg = K[:, :, idx]
        Vg = V[:, :, idx]
        s_scores = jnp.einsum('bhsd,bhskd->bhsk', Q, Kg) * scale
        s_scores = jnp.where(prior_index_mask[:Ss][None, None], s_scores, jnp.asarray(-jnp.inf, x.dtype))
        sparse_out = jnp.einsum('bhsk,bhskd->bhsd', jax.nn.softmax(s_scores, axis=-1), Vg)
        out = jnp.where(use_sparse[:, None, None, None], sparse_out, dense_out)
        out = out.transpose(0, 2, 1, 3).reshape(Bb, Ss, Dd)
        return out @ Wo.T + bo

    def _L2_cond_ref(hidden_states, expert_ids, wi, wo, common_wi_a, common_wi_b, common_wo_a, common_wo_b, experts_wi_a, experts_wi_b, experts_wo_a, experts_wo_b):
        import jax, jax.numpy as jnp
        import numpy as np
        B, S, D, F = (32, 64, 128, 512)
        R_COMMON, R_DOMAIN, E = (16, 16, 8)
        ALPHA = 2.0

        def _expert_lora(x, expert_ids, Wa, Wb):
            Ab = Wa[expert_ids]
            Bb = Wb[expert_ids]
            low = jnp.einsum('bsd,brd->bsr', x, Ab)
            return ALPHA * jnp.einsum('bsr,bor->bso', low, Bb)
        x = hidden_states
        hidden_i = jnp.einsum('bsd,fd->bsf', x, wi)
        hidden_i += ALPHA * jnp.einsum('bsr,fr->bsf', jnp.einsum('bsd,rd->bsr', x, common_wi_a), common_wi_b)
        hidden_i += _expert_lora(x, expert_ids, experts_wi_a, experts_wi_b)
        hidden_i = jax.nn.relu(hidden_i)
        hidden_o = jnp.einsum('bsf,df->bsd', hidden_i, wo)
        hidden_o += ALPHA * jnp.einsum('bsr,dr->bsd', jnp.einsum('bsf,rf->bsr', hidden_i, common_wo_a), common_wo_b)
        hidden_o += _expert_lora(hidden_i, expert_ids, experts_wo_a, experts_wo_b)
        return hidden_o

    def _L3_cond_ref(x, indices, fc1_w, fc1_b, fc2_w, fc2_b, experts_w, experts_b):
        import jax, jax.numpy as jnp
        import numpy as np
        B, N, DIM = (32, 128, 128)
        HID = 512
        PART = 32
        OUT = 128
        SHARED = OUT - PART
        E = 16
        h = jax.nn.gelu(jnp.einsum('bnd,hd->bnh', x, fc1_w) + fc1_b, approximate=False)
        shared = jnp.einsum('bnh,sh->bns', h, fc2_w) + fc2_b
        We = experts_w[indices]
        be = experts_b[indices]
        expert_x = jnp.einsum('bnh,bph->bnp', h, We) + be[:, None, :]
        return jnp.concatenate([shared, expert_x], axis=-1)
    x = x + _L0_cond_ref(x, L0_cond_W1, L0_cond_b1, L0_cond_v, itok_B_0_2)
    x = x + _L1_cond_ref(x, mask_SxS_bk0, itok_Sx32_0_1023, mask_Sx32_bk1, condB_uprev[:, None], L1_cond_Wq, L1_cond_bq, L1_cond_Wk, L1_cond_bk, L1_cond_Wv, L1_cond_bv, L1_cond_Wo, L1_cond_bo)
    x = x + _L2_cond_ref(x, itok_B_0_7, L2_cond_wi, L2_cond_wo, L2_cond_common_wi_a, L2_cond_common_wi_b, L2_cond_common_wo_a, L2_cond_common_wo_b, L2_cond_experts_wi_a, L2_cond_experts_wi_b, L2_cond_experts_wo_a, L2_cond_experts_wo_b)
    x = x + _L3_cond_ref(x, itok_B_0_15, L3_cond_fc1_w, L3_cond_fc1_b, L3_cond_fc2_w, L3_cond_fc2_b, L3_cond_experts_w, L3_cond_experts_b)
    return x

_drawn_inputs = setup_inputs


def setup_inputs(seed=0):
    import zlib

    import numpy as np

    out = dict(_drawn_inputs(seed))
    spreads = {'L1_cond_bq': (0.0, 0.1),
     'L1_cond_bk': (0.0, 2.0),
     'L1_cond_bv': (0.0, 0.1),
     'L1_cond_bo': (0.0, 0.1),
     'L3_cond_fc1_b': (0.0, 2.0),
     'L3_cond_fc2_b': (0.0, 0.8),
     'L3_cond_experts_b': (0.0, 0.8)}
    factors = {'L0_cond_b1': 64.0}
    for name, (base, spread) in spreads.items():
        noise = np.random.default_rng([zlib.crc32(name.encode()), seed]).standard_normal(out[name].shape)
        drawn = base * np.exp(spread * noise) if base else spread * noise
        out[name] = jnp.asarray(drawn.astype(out[name].dtype))
    for name, factor in factors.items():
        out[name] = (out[name] * factor).astype(out[name].dtype)
    return out
```

```python
from contextlib import ExitStack

import concourse.bass as bass
from concourse import mybir

F32 = mybir.dt.float32
I32 = mybir.dt.int32
U8 = mybir.dt.uint8
ALU = mybir.AluOpType
ACT = mybir.ActivationFunctionType
AX = mybir.AxisListType

P = 128
B = 128
S = 32
D = 128
Q4 = P // S
G = 4
TOK = G * P
NBLK = B * S // TOK
ROWS = G * Q4
TILES = B // Q4
A0 = 32
H = 16
DH = D // H
HG = 4
H4 = H // HG
F = 512
FC = F // P
E2 = 8
E3 = 16
PART = 32
SHARED = D - PART
SCALE = DH ** -0.5
NEG = -1e30
LAM_MAX, LAM_RATE, ALPHA = 10.0, 5.0, 2.0

I_TYPE, I_E2, I_E3, I_IDX, I_END = 0, 32, 160, 288, 320
C_SIGN, C_IOTA, C_U, C_HEAD, C_BQ, C_BK, C_FC1B, C_E2, C_E3, C_BO, C_BV, C_B1, C_END = (
    0, 32, 64, 96, 100, 104, 108, 112, 113, 114, 115, 116, 117)


def cond_resid_kernel(nc, xt, xn, ints, bools, cols, w1, vrep, wq, wk, wv, wo, wit, wot, cwia, cwibt,
                      cwoa, cwobt, ewiat, ewib, ewoat, ewob, fc1t, fc2t, e3t, fb3, ident_in, out):
    with ExitStack() as ctx:
        def sb(name, shape, dt=F32):
            return ctx.enter_context(nc.sbuf_tensor(name, shape, dt))

        def bank(name):
            return ctx.enter_context(nc.psum_tensor(name, [P, 512], F32))

        def sem(name):
            return ctx.enter_context(nc.semaphore(name))

        ints_s = sb("ints_s", [P, I_END], I32)
        bools_s = sb("bools_s", [P, 2 * S // 4], I32)
        cols_s = sb("cols_s", [P, C_END])
        w1_s, vrep_s = sb("w1_s", [D, A0]), sb("vrep_s", [A0, P])
        wq_s, wk_s, wv_s, wo_s = (sb(n, [D, D]) for n in ("wq_s", "wk_s", "wv_s", "wo_s"))
        wit_s = sb("wit_s", [D, F])
        wot_s = sb("wot_s", [P, FC, D])
        cwia_s, cwibt_s = sb("cwia_s", [16, D]), sb("cwibt_s", [16, F])
        cwoa_s, cwobt_s = sb("cwoa_s", [16, F]), sb("cwobt_s", [16, D])
        ewiat_s = sb("ewiat_s", [D, P])
        ewib_s = sb("ewib_s", [P, F])
        ewoat_s = sb("ewoat_s", [P, FC, P])
        ewob_s = sb("ewob_s", [P, D])
        fc1t_s = sb("fc1t_s", [D, F])
        e3t_s = sb("e3t_s", [P, E3, FC, PART])
        fb3_s = sb("fb3_s", [E3 + 1, D])
        ident = sb("ident", [P, P])

        intf = sb("intf", [P, I_END])
        neg_c = sb("neg_c", [P, TILES])
        masked = sb("masked", [P, TILES, S])
        cnt = sb("cnt", [P, TILES])
        idxm = sb("idxm", [P, S])
        mk = sb("mk", [P, 2 * S])
        hits = sb("hits", [P, S, S])
        ctab = sb("ctab", [P, S])
        ltab = sb("ltab", [P, S])
        ztab = sb("ztab", [P, S])
        ntab = sb("ntab", [P, S])
        lam = sb("lam", [P, TILES])
        hi = sb("hi", [P, TILES])
        lo = sb("lo", [P, TILES])
        cd = sb("cd", [P, TILES])
        bias = sb("bias", [P, TILES, S])
        btmp = sb("btmp", [P, TILES, S])
        oh2 = sb("oh2", [P, B])
        oh3 = sb("oh3", [E3 + 1, B])
        e3i = sb("e3i", [P, B], I32)
        fbias = sb("fbias", [D, B])
        bo_eff = sb("bo_eff", [D, 1])

        xT, xN = sb("xT", [D, TOK]), sb("xN", [P, G, D])
        th = sb("th", [A0, TOK])
        l0s = sb("l0s", [P, G, S])
        l0e = sb("l0e", [P, G, S])
        l0m, l0d, l0r = sb("l0m", [P, G]), sb("l0d", [P, G]), sb("l0r", [P, G])
        l0c = sb("l0c", [P, G])
        poolP = sb("poolP", [P, G, P])
        x1T = sb("x1T", [D, TOK])
        qb = sb("qb", [P, HG, G, P])
        kb = sb("kb", [P, HG, H4, G, S])
        vb = sb("vb", [P, G, H, Q4, DH + 1])
        sc = sb("sc", [P, 2, H, S])
        rmax = sb("rmax", [P, 2, H])
        ex = sb("ex", [P, 2, H, S])
        pt = sb("pt", [P, 2, H, S])
        rc = sb("rc", [P, 2, HG, Q4])
        on = sb("on", [P, 2, Q4, HG, DH])
        oT = sb("oT", [P, G, P])
        x2T = sb("x2T", [D, TOK])

        lowm = sb("lowm", [P, TOK])
        lowm2 = sb("lowm2", [P, TOK])
        hid = sb("hid", [P, FC, TOK])
        x3T = sb("x3T", [D, TOK])
        x3b = sb("x3b", [D, TOK])
        hT = sb("hT", [P, FC, TOK])
        rw = sb("rw", [P, ROWS, FC, D])
        o_s = sb("o_s", [P, G, D])

        pA0, pA1, pS0, pS1, pV, pB0, pB1, pB2 = (
            bank(n) for n in ("pA0", "pA1", "pS0", "pS1", "pV", "pB0", "pB1", "pB2"))
        pS = [pS0, pS1]

        ld_small, ld_attn, ld_ffn, ld_rw = sem("ld_small"), sem("ld_attn"), sem("ld_ffn"), sem("ld_rw")
        ld_xT, ld_xN, st_out = sem("ld_xT"), sem("ld_xN"), sem("st_out")
        prep = sem("prep")
        prep_act, prep_pe, prep_pool = sem("prep_act"), sem("prep_pe"), sem("prep_pool")
        h_ps, th_sb, s_ps = sem("h_ps"), sem("th_sb"), sem("s_ps")
        l0_step, l0_exp, pool_ps, x1_sb = sem("l0_step"), sem("l0_exp"), sem("pool_ps"), sem("x1_sb")
        q_ps, k_ps, v_ps = sem("q_ps"), sem("k_ps"), sem("v_ps")
        q_sb, k_sb, v_sb = sem("q_sb"), sem("k_sb"), sem("v_sb")
        sc_ps, sc_sb, mx_sb = sem("sc_ps"), sem("sc_sb"), sem("mx_sb")
        sub_sb, ex_sb, pt_sb, pv_ps = sem("sub_sb"), sem("ex_sb"), sem("pt_sb"), sem("pv_ps")
        rc_sb, on_sb, o_sb = sem("rc_sb"), sem("on_sb"), sem("o_sb")
        wo_ps, x2_sb = sem("wo_ps"), sem("x2_sb")
        low_ps, low_sb, low2_ps, low2_sb = sem("low_ps"), sem("low_sb"), sem("low2_ps"), sem("low2_sb")
        hid_ps, hid_sb = sem("hid_ps"), sem("hid_sb")
        out_ps, x3_sb, x3b_sb = sem("out_ps"), sem("x3_sb"), sem("x3b_sb")
        g_ps, g_sb = sem("g_ps"), sem("g_sb")
        rw_sb, fin_ps, fin_sb = sem("rw_sb"), sem("fin_ps"), sem("fin_sb")

        def at(eng, s, value):
            if isinstance(value, int) and value <= 0:
                return
            eng.wait_ge(s, value)

        N_SMALL, N_ATTN, N_FFN = 3, 6, 13
        PREP_VEC = [0]

        block = ctx.enter_context(nc.Block())

        @block.sync
        def _(sp):
            sp.dma_start(ints_s[:, :], ints).then_inc(ld_small, 16)
            sp.dma_start(bools_s[:, :], bools).then_inc(ld_small, 16)
            sp.dma_start(cols_s[:, :], cols).then_inc(ld_small, 16)

            def load_x(i):
                at(sp, x1_sb, i)
                sp.dma_start(xT[:, :], xt[i]).then_inc(ld_xT, 16)
                at(sp, pool_ps, i)
                sp.dma_start(xN[:, :, :], xn[i]).then_inc(ld_xN, 16)

            def store(i):
                at(sp, fin_sb, i + 2)
                sp.dma_start(out[i], o_s[:, :, :]).then_inc(st_out, 16)

            sp.sem_inc(st_out, 16)
            load_x(0)
            for dst, src in ((w1_s, w1), (vrep_s, vrep), (wq_s, wq), (wk_s, wk), (wv_s, wv), (wo_s, wo)):
                sp.dma_start(dst[:, :], src).then_inc(ld_attn, 16)
            for dst, src in ((cwia_s[:, :], cwia), (cwibt_s[:, :], cwibt), (cwoa_s[:, :], cwoa),
                             (cwobt_s[:, :], cwobt), (fb3_s[:, :], fb3), (ident[:, :], ident_in),
                             (wit_s[:, :], wit), (wot_s[:, :, :], wot),
                             (ewiat_s[:, :], ewiat), (ewib_s[:, :], ewib), (ewoat_s[:, :, :], ewoat),
                             (ewob_s[:, :], ewob), (fc1t_s[:, :], fc1t)):
                sp.dma_start(dst, src).then_inc(ld_ffn, 16)
            sp.dma_start(e3t_s[:, :, :, :], e3t).then_inc(ld_rw, 16)
            for r in range(ROWS):
                sp.dma_start(rw[:, r, :, 0:SHARED], fc2t).then_inc(ld_rw, 16)
            load_x(1)
            with sp.Fori(0, NBLK - 2) as i:
                load_x(i + 2)
                store(i)
            store(NBLK - 2)
            store(NBLK - 1)
            sp.wait_ge(st_out, 16 * (NBLK + 1))

        @block.gpsimd
        def _(pool):
            pool.memset(poolP[:, :, :], 0.0).then_inc(prep_pool, 1)
            pool.memset(qb[:, :, :, :], 0.0).then_inc(prep_pool, 1)
            pool.memset(vb[:, :, :, :, :], 0.0).then_inc(prep_pool, 1)
            pool.wait_ge(prep_pool, 3)
            for q in range(Q4):
                pool.memset(vb[S * q:S * q + S, :, :, q, DH:DH + 1], 1.0).then_inc(prep_pool, 1)

            def subtract_max(i, g):
                at(pool, mx_sb, G * i + g + 1)
                pool.tensor_tensor(sc[:, g % 2, :, :], sc[:, g % 2, :, :],
                                   rmax[:, g % 2, :].unsqueeze(2).to_broadcast([P, H, S]),
                                   ALU.subtract).then_inc(sub_sb, 1)

            def expert_weights(i):
                at(pool, fin_ps, i + 1)
                for r in range(ROWS):
                    e = pool.value_load(e3i[0:1, bass.ds(ROWS * i + r, 1)], min_val=0, max_val=E3 - 1)
                    pool.tensor_copy(rw[:, r, :, SHARED:D],
                                     e3t_s[:, bass.ds(e, 1), :, :].rearrange("p o c n -> p (o c) n"))\
                        .then_inc(rw_sb, 1)

            for g in range(G):
                subtract_max(0, g)
            pool.wait_ge(ld_rw, 16 * (1 + ROWS))
            pool.wait_ge(prep, P_E3)
            with pool.Fori(0, NBLK - 1) as i:
                expert_weights(i)
                for g in range(G):
                    subtract_max(i + 1, g)
            expert_weights(NBLK - 1)

        @block.scalar
        def _(act):
            act.wait_ge(ld_small, 16 * N_SMALL)
            act.activation(lam[:, :], cols_s[:, C_U:C_U + TILES], ACT.Exp, scale=-LAM_RATE).then_inc(prep_act, 1)
            act.wait_ge(prep, P_COUNT)
            act.activation(ltab[:, :], ctab[:, :], ACT.Ln).then_inc(prep_act, 1)

            def tanh(i):
                at(act, h_ps, i + 1)
                act.activation(th[:, :], pA0[0:A0, :], ACT.Tanh, bias=cols_s[0:A0, C_B1:C_B1 + 1]).then_inc(th_sb, 1)

            def l0_exps(i):
                at(act, l0_step, L0_STEPS * i + 6)
                act.activation(l0e[:, :, :], l0s[:, :, :], ACT.Exp).then_inc(l0_exp, 1)

            def values(i):
                at(act, v_ps, i + 1)
                for q in range(Q4):
                    part = slice(S * q, S * q + S)
                    act.activation(vb[part, :, :, q, 0:DH].rearrange("p g h d -> p (g h) d"),
                                   pV[part, :].rearrange("p (n d) -> p n d", d=DH), ACT.Copy).then_inc(v_sb, 1)

            def exps(i, g):
                t = G * i + g
                at(act, sub_sb, t + 1)
                at(act, pt_sb, t - 1)
                act.activation(ex[:, g % 2, :, :], sc[:, g % 2, :, :], ACT.Exp).then_inc(ex_sb, 1)

            def relu(i, c):
                at(act, hid_ps, FC * i + c + 1)
                act.activation(hid[:, c, :], [pB1, pB2, pB0, pB1][c][:, :], ACT.Relu).then_inc(hid_sb, 1)

            def gelu(i, c):
                at(act, g_ps, FC * i + c + 1)
                act.activation(hT[:, c, :], [pB1, pB2, pB0, pB1][c][:, :], ACT.Gelu,
                               bias=cols_s[:, C_FC1B + c:C_FC1B + c + 1]).then_inc(g_sb, 1)

            def result(i):
                at(act, fin_ps, i + 2)
                at(act, st_out, 16 * (i + 1))
                act.activation(o_s[:, :, :], pB2[:, :].rearrange("p (g d) -> p g d", g=G), ACT.Copy).then_inc(fin_sb, 1)

            act.wait_ge(prep_pool, 3 + Q4)
            act.sem_inc(fin_sb, 1)
            tanh(0)
            l0_exps(0)
            values(0)
            for g in range(G):
                exps(0, g)
            with act.Fori(0, NBLK - 1) as i:
                tanh(i + 1)
                relu(i, 0)
                l0_exps(i + 1)
                for c in range(1, FC):
                    relu(i, c)
                values(i + 1)
                for g in range(G):
                    exps(i + 1, g)
                for c in range(FC):
                    gelu(i, c)
                result(i)
            for c in range(FC):
                relu(NBLK - 1, c)
            for c in range(FC):
                gelu(NBLK - 1, c)
            result(NBLK - 1)

        @block.tensor
        def _(pe):
            mm = pe.matmul

            def scorer_in(i):
                at(pe, ld_xT, 16 * (i + 1))
                at(pe, k_sb, HG * i)
                mm(pA0[0:A0, :], w1_s[:, :], xT[:, :], start=True, stop=True).then_inc(h_ps, 1)

            def scorer_out(i):
                at(pe, th_sb, i + 1)
                at(pe, x2_sb, i)
                mm(pA1[:, :], vrep_s[:, :], th[:, :], start=True, stop=True).then_inc(s_ps, 1)

            def pooling(i):
                at(pe, ld_xN, 16 * (i + 1))
                at(pe, l0_step, L0_STEPS * (i + 1))
                for g in range(G):
                    last = mm(pA0[:, P * g:P * g + P], xN[:, g, :], poolP[:, g, :], start=True, stop=True)
                last.then_inc(pool_ps, 1)

            def project(i):
                at(pe, x1_sb, i + 1)
                rows = x1T[:, :].rearrange("p (g q s) -> p g q s", g=G, q=Q4)
                for ps, w, done in ((pA1, wq_s, q_ps), (pA0, wk_s, k_ps)):
                    for hg in range(HG):
                        for q in range(Q4):
                            last = mm(ps[S * q:S * q + S, P * hg:P * hg + P], w[:, S * hg:S * hg + S],
                                      rows[:, :, q, :], start=True, stop=True)
                    last.then_inc(done, 1)
                at(pe, on_sb, G * i)
                for g in range(G):
                    last = mm(pV[:, P * g:P * g + P], x1T[:, P * g:P * g + P], wv_s[:, :], start=True, stop=True)
                last.then_inc(v_ps, 1)

            def scores(i, g):
                if g == 0:
                    at(pe, q_sb, Q4 * (i + 1))
                    at(pe, k_sb, HG * (i + 1))
                at(pe, sc_sb, G * i + g - 1)
                for hg in range(HG):
                    last = mm(pS[g % 2][:, P * hg:P * hg + P], qb[:, hg, g, :], kb[:, hg, :, g, :],
                              start=True, stop=True)
                last.then_inc(sc_ps, 1)

            def weigh(i, g):
                at(pe, pt_sb, G * i + g + 1)
                if g == 0:
                    at(pe, v_sb, Q4 * (i + 1))
                if g == 2:
                    at(pe, on_sb, G * i + 2)
                w = Q4 * (DH + 1)
                for hg in range(HG):
                    for h4 in range(H4):
                        h = H4 * hg + h4
                        at_col = (g % 2) * HG * w + hg * w
                        last = mm(pV[S * h4:S * h4 + S, at_col:at_col + w], pt[:, g % 2, h, :],
                                  vb[:, g, h, :, :], start=True, stop=True)
                last.then_inc(pv_ps, 1)

            def attn_out(i):
                at(pe, o_sb, G // 2 * (i + 1))
                mm(pA1[:, :], wo_s[:, :], oT[:, :, :], start=True, stop=True).then_inc(wo_ps, 1)

            def low(i):
                at(pe, x2_sb, i + 1)
                mm(pB0[:, :], ewiat_s[:, :], x2T[:, :], start=True, stop=True).then_inc(low_ps, 1)

            def hidden(i, c):
                ps = [pB1, pB2, pB0, pB1][c]
                if c == 1:
                    at(pe, fin_sb, i + 1)
                if c == 2:
                    at(pe, low_sb, i + 1)
                if c == 3:
                    at(pe, hid_sb, FC * i + 1)
                mm(ps[:, :], wit_s[:, P * c:P * c + P], x2T[:, :], start=True, stop=False)
                if c == 0:
                    return
                hidden_expert(i, c)

            def hidden_expert(i, c):
                ps = [pB1, pB2, pB0, pB1][c]
                if c == 0:
                    at(pe, low_sb, i + 1)
                mm(ps[:, :], ewib_s[:, P * c:P * c + P], lowm[:, :], start=False, stop=True).then_inc(hid_ps, 1)

            def low2(i):
                for c in range(FC):
                    at(pe, hid_sb, FC * i + (c + 1 if c != 0 else 2))
                    last = mm(pB2[:, :], ewoat_s[:, c, :], hid[:, c, :], start=(c == 0), stop=(c == FC - 1))
                last.then_inc(low2_ps, 1)

            def out2(i):
                at(pe, hid_sb, FC * (i + 1))
                for c in range(FC):
                    mm(pB0[:, :], wot_s[:, c, :], hid[:, c, :], start=(c == 0), stop=False)
                at(pe, low2_sb, i + 1)
                mm(pB0[:, :], ewob_s[:, :], lowm2[:, :], start=False, stop=True).then_inc(out_ps, 1)

            def fc1(i, c):
                ps = [pB1, pB2, pB0, pB1][c]
                if c == 0:
                    at(pe, x3_sb, i + 1)
                if c == 3:
                    at(pe, g_sb, FC * i + 1)
                mm(ps[:, :], fc1t_s[:, P * c:P * c + P], x3T[:, :], start=True, stop=True).then_inc(g_ps, 1)

            def final(i, g):
                if g == 0:
                    at(pe, g_sb, FC * (i + 1))
                    at(pe, rw_sb, ROWS * (i + 1))
                    at(pe, x3b_sb, i + 1)
                for c in range(FC + 1):
                    for q in range(Q4):
                        tok = slice(P * g + S * q, P * g + S * q + S)
                        if c < FC:
                            lhs, rhs = hT[:, c, tok], rw[:, Q4 * g + q, c, :]
                        else:
                            lhs, rhs = x3b[:, tok], ident[:, :]
                        last = mm(pB2[S * q:S * q + S, P * g:P * g + P], lhs, rhs, start=(c == 0), stop=(c == FC))
                if g == G - 1:
                    last.then_inc(fin_ps, 1)

            pe.wait_ge(ld_ffn, 16 * N_FFN)
            mm(pB0[:, :], cwia_s[:, :], cwibt_s[:, :], start=True, stop=True).then_inc(prep_pe, 1)
            for c in range(FC):
                last = mm(pB1[:, P * c:P * c + P], cwoa_s[:, P * c:P * c + P], cwobt_s[:, :], start=True, stop=True)
            last.then_inc(prep_pe, 1)
            pe.wait_ge(ld_attn, 16 * N_ATTN)
            pe.wait_ge(ld_small, 16 * N_SMALL)
            mm(pB2[:, 0:1], wo_s[:, :], cols_s[:, C_BV:C_BV + 1], start=True, stop=True).then_inc(prep_pe, 1)
            pe.wait_ge(prep, P_E3)
            mm(pS0[:, 0:B], fb3_s[:, :], oh3[:, :], start=True, stop=True).then_inc(prep_pe, 1)

            pe.sem_inc(fin_ps, 1)
            scorer_in(0)
            scorer_out(0)
            pe.wait_ge(prep_pool, 3 + Q4)
            pooling(0)
            project(0)
            pe.wait_ge(prep, P_ALL)
            scores(0, 0)
            scores(0, 1)
            weigh(0, 0)
            scores(0, 2)
            weigh(0, 1)
            scores(0, 3)
            weigh(0, 2)
            weigh(0, 3)
            attn_out(0)
            with pe.Fori(0, NBLK - 1) as i:
                scorer_in(i + 1)
                low(i)
                hidden(i, 0)
                scorer_out(i + 1)
                hidden_expert(i, 0)
                hidden(i, 1)
                hidden(i, 2)
                pooling(i + 1)
                hidden(i, 3)
                project(i + 1)
                low2(i)
                scores(i + 1, 0)
                scores(i + 1, 1)
                out2(i)
                weigh(i + 1, 0)
                scores(i + 1, 2)
                weigh(i + 1, 1)
                scores(i + 1, 3)
                fc1(i, 0)
                fc1(i, 1)
                weigh(i + 1, 2)
                fc1(i, 2)
                weigh(i + 1, 3)
                fc1(i, 3)
                attn_out(i + 1)
                for g in range(G):
                    final(i, g)
            last_i = NBLK - 1
            low(last_i)
            hidden(last_i, 0)
            hidden_expert(last_i, 0)
            for c in range(1, FC):
                hidden(last_i, c)
            low2(last_i)
            out2(last_i)
            for c in range(FC):
                fc1(last_i, c)
            for g in range(G):
                final(last_i, g)

        @block.vector
        def _(dve):
            tt, ts, stt = dve.tensor_tensor, dve.tensor_scalar, dve.scalar_tensor_tensor

            def step(ins):
                PREP_VEC[0] += 1
                ins.then_inc(prep, 1)
                dve.wait_ge(prep, PREP_VEC[0])

            def wrap(col, width, n):
                x, t = intf[:, col:col + width], btmp[:, 0:4, :].rearrange("p a b -> p (a b)")[:, 0:width]
                step(ts(t, x, 0.0, float(n), ALU.is_lt, ALU.mult))
                step(tt(x, x, t, ALU.add))
                step(ts(x, x, 0.0, float(n - 1), ALU.max, ALU.min))

            dve.wait_ge(ld_small, 16 * N_SMALL)
            step(dve.tensor_copy(intf[:, :], ints_s[:, :]))
            step(dve.tensor_copy(mk[:, :], bools_s[:, :].bitcast(U8)))
            wrap(I_IDX, S, S)
            wrap(I_E2, B, E2)
            wrap(I_E3, B, E3)
            step(dve.tensor_copy(e3i[:, :], intf[:, I_E3:I_E3 + B]))
            step(ts(oh3[:, :], intf[0:E3 + 1, I_E3:I_E3 + B], cols_s[0:E3 + 1, C_E3:C_E3 + 1], None, ALU.is_equal))
            assert PREP_VEC[0] == P_E3
            step(ts(oh2[:, :], intf[:, I_E2:I_E2 + B], cols_s[:, C_E2:C_E2 + 1], ALPHA, ALU.is_equal, ALU.mult))
            step(stt(idxm[:, :], intf[:, I_IDX:I_IDX + S], 1.0, mk[:, S:2 * S], ALU.add, ALU.mult))
            step(ts(idxm[:, :], idxm[:, :], -1.0, None, ALU.add))
            step(tt(hits[:, :, :], idxm[:, :].unsqueeze(1).to_broadcast([P, S, S]),
                    cols_s[:, C_IOTA:C_IOTA + S].unsqueeze(2).to_broadcast([P, S, S]), ALU.is_equal))
            step(dve.tensor_reduce(ntab[:, :], hits[:, :, :], AX.X, ALU.add))
            step(ts(ctab[:, :], ntab[:, :], 1.0, None, ALU.max))
            assert PREP_VEC[0] == P_COUNT
            step(ts(ztab[:, :], ntab[:, :], -0.5, -2 * NEG, ALU.add, ALU.mult))
            step(ts(ntab[:, :], mk[:, 0:S], -1.0, 1.0, ALU.mult, ALU.add))
            step(ts(cnt[:, :], intf[:, I_TYPE:I_TYPE + TILES], 0.0, None, ALU.is_equal))
            step(stt(neg_c[:, :], intf[:, I_TYPE:I_TYPE + TILES], 1.0, cnt[:, :], ALU.is_equal, ALU.subtract))
            step(tt(masked[:, :, :], cols_s[:, C_SIGN:C_SIGN + S].unsqueeze(1).to_broadcast([P, TILES, S]),
                    neg_c[:, :].unsqueeze(2).to_broadcast([P, TILES, S]), ALU.is_equal))
            step(dve.tensor_reduce(cnt[:, :], masked[:, :, :], AX.X, ALU.add))
            step(ts(cnt[:, :], cnt[:, :], -1.0, float(S), ALU.mult, ALU.add))
            dve.wait_ge(prep_act, 2)
            step(ts(lam[:, :], lam[:, :], LAM_MAX, None, ALU.mult))
            step(ts(hi[:, :], lam[:, :], 1.0, -2 * NEG, ALU.is_ge, ALU.mult))
            step(ts(lo[:, :], hi[:, :], -1.0, None, ALU.mult))
            step(stt(cd[:, :], lam[:, :], 1.0, lam[:, :], ALU.is_lt, ALU.mult))
            step(ts(cd[:, :], cd[:, :], -1.0, None, ALU.mult))
            step(tt(ltab[:, :], ltab[:, :], ztab[:, :], ALU.min))

            def by_token(x):
                return x[:, :].unsqueeze(1).to_broadcast([P, TILES, S])

            def by_tile(x):
                return x[:, :].unsqueeze(2).to_broadcast([P, TILES, S])

            step(tt(bias[:, :, :], by_token(ltab), by_tile(lo), ALU.max))
            step(tt(bias[:, :, :], bias[:, :, :], by_tile(hi), ALU.min))
            step(tt(btmp[:, :, :], by_token(ntab), by_tile(cd), ALU.mult))
            step(tt(bias[:, :, :], bias[:, :, :], btmp[:, :, :], ALU.add))
            dve.wait_ge(prep_pe, 4)
            step(stt(wit_s[:, :], pB0[:, :], ALPHA, wit_s[:, :], ALU.mult, ALU.add))
            wot_f = wot_s[:, :, :].rearrange("p c d -> p (c d)")
            step(stt(wot_f, pB1[:, :], ALPHA, wot_f, ALU.mult, ALU.add))
            step(tt(bo_eff[:, :], pB2[:, 0:1], cols_s[:, C_BO:C_BO + 1], ALU.add))
            step(dve.tensor_copy(fbias[:, :], pS0[:, 0:B]))
            assert PREP_VEC[0] == P_ALL
            dve.wait_ge(prep_pool, 3 + Q4)

            def pool_weights(i, part):
                n = L0_STEPS * i
                if part == 0:
                    at(dve, s_ps, i + 1)
                    tok = pA1[:, :].rearrange("p (g q l) -> p g q l", g=G, q=Q4)
                    for q in range(Q4):
                        k = slice(S * q, S * q + S)
                        stt(l0s[k, :, :], masked[k, bass.ds(G * i, G), :], NEG, tok[k, :, q, :],
                            ALU.mult, ALU.add).then_inc(l0_step, 1)
                    at(dve, l0_step, n + 4)
                    dve.tensor_reduce(l0m[:, :], l0s[:, :, :], AX.X, ALU.max).then_inc(l0_step, 1)
                    at(dve, l0_step, n + 5)
                    tt(l0s[:, :, :], l0s[:, :, :], l0m[:, :].unsqueeze(2).to_broadcast([P, G, S]),
                       ALU.subtract).then_inc(l0_step, 1)
                    return
                at(dve, l0_exp, i + 1)
                dve.tensor_reduce(l0d[:, :], l0e[:, :, :], AX.X, ALU.add).then_inc(l0_step, 1)
                at(dve, l0_step, n + 7)
                tt(l0r[:, :], l0d[:, :], cnt[:, bass.ds(G * i, G)], ALU.mult).then_inc(l0_step, 1)
                at(dve, l0_step, n + 8)
                dve.reciprocal(l0c[:, :], l0r[:, :]).then_inc(l0_step, 1)
                at(dve, l0_step, n + 9)
                tt(l0e[:, :, :], l0e[:, :, :], l0c[:, :].unsqueeze(2).to_broadcast([P, G, S]),
                   ALU.mult).then_inc(l0_step, 1)
                at(dve, l0_step, n + 10)
                for q in range(Q4):
                    k = slice(S * q, S * q + S)
                    dve.transpose(poolP[k, :, k], l0e[k, :, :]).then_inc(l0_step, 1)

            def x1(i):
                at(dve, pool_ps, i + 1)
                tt(x1T[:, :], pA0[:, :], xT[:, :], ALU.add).then_inc(x1_sb, 1)

            def queries_keys(i):
                at(dve, q_ps, i + 1)
                for q in range(Q4):
                    k = slice(S * q, S * q + S)
                    tt(qb[k, :, :, k], pA1[k, :].rearrange("p (a g s) -> p a g s", a=HG, g=G),
                       cols_s[k, C_BQ:C_BQ + HG].unsqueeze(2).unsqueeze(3).to_broadcast([S, HG, G, S]),
                       ALU.add).then_inc(q_sb, 1)
                at(dve, k_ps, i + 1)
                for hg in range(HG):
                    stt(kb[:, hg, :, :, :].rearrange("p h g t -> p h (g t)"), pA0[:, P * hg:P * hg + P].unsqueeze(1).to_broadcast([P, H4, P]),
                        cols_s[:, C_BK + hg:C_BK + hg + 1],
                        cols_s[:, C_HEAD:C_HEAD + H4].unsqueeze(2).to_broadcast([P, H4, P]),
                        ALU.add, ALU.mult).then_inc(k_sb, 1)

            def score_max(i, g):
                t = G * i + g
                at(dve, sc_ps, t + 1)
                at(dve, ex_sb, t - 1)
                stt(sc[:, g % 2, :, :], pS[g % 2][:, :].rearrange("p (h t) -> p h t", t=S), SCALE,
                    bias[:, bass.ds(t, 1), :].to_broadcast([P, H, S]), ALU.mult, ALU.add).then_inc(sc_sb, 1)
                at(dve, sc_sb, t + 1)
                dve.tensor_reduce(rmax[:, g % 2, :], sc[:, g % 2, :, :], AX.X, ALU.max).then_inc(mx_sb, 1)

            def turn(i, g):
                t = G * i + g
                at(dve, ex_sb, t + 1)
                at(dve, pv_ps, t - 1)
                dve.transpose(pt[:, g % 2, :, :], ex[:, g % 2, :, :]).then_inc(pt_sb, 1)

            def normalise(i, pair):
                n = G // 2 * i + pair
                at(dve, pv_ps, 2 * n + 2)
                sums = pV[:, 0:2 * H * (DH + 1)].rearrange("p (n d) -> p n d", d=DH + 1)
                dve.reciprocal(rc[:, :, :, :].rearrange("p t a q -> p (t a q)"), sums[:, :, DH]).then_inc(rc_sb, 1)
                at(dve, rc_sb, n + 1)
                for t in range(2):
                    tt(on[:, t, :, :, :].rearrange("p q a d -> p a q d"),
                       sums[:, H * t:H * t + H, 0:DH].rearrange("p (a q) d -> p a q d", q=Q4),
                       rc[:, t, :, :].unsqueeze(3).to_broadcast([P, HG, Q4, DH]), ALU.mult).then_inc(on_sb, 1)
                at(dve, on_sb, 2 * n + 2)
                dve.transpose(oT[:, 2 * pair:2 * pair + 2, :],
                              on[:, :, :, :, :].rearrange("p t q a d -> p t (q a d)")).then_inc(o_sb, 1)

            def x2(i):
                at(dve, wo_ps, i + 1)
                stt(x2T[:, :], pA1[:, :], bo_eff[:, 0:1], x1T[:, :], ALU.add, ALU.add).then_inc(x2_sb, 1)

            def rows_of(x, i):
                return x[:, bass.ds(ROWS * i, ROWS)].unsqueeze(2).to_broadcast([P, ROWS, S])

            def by_row(x):
                return x[:, :].rearrange("p (r s) -> p r s", s=S)

            def mask_low(i):
                at(dve, low_ps, i + 1)
                tt(by_row(lowm), by_row(pB0), rows_of(oh2, i), ALU.mult).then_inc(low_sb, 1)

            def mask_low2(i):
                at(dve, low2_ps, i + 1)
                tt(by_row(lowm2), by_row(pB2), rows_of(oh2, i), ALU.mult).then_inc(low2_sb, 1)

            def x3(i):
                at(dve, out_ps, i + 1)
                tt(x3T[:, :], pB0[:, :], x2T[:, :], ALU.add).then_inc(x3_sb, 1)
                at(dve, x3_sb, i + 1)
                tt(by_row(x3b), by_row(x3T), rows_of(fbias, i), ALU.add).then_inc(x3b_sb, 1)

            pool_weights(0, 0)
            pool_weights(0, 1)
            x1(0)
            queries_keys(0)
            score_max(0, 0)
            score_max(0, 1)
            turn(0, 0)
            score_max(0, 2)
            turn(0, 1)
            score_max(0, 3)
            turn(0, 2)
            normalise(0, 0)
            turn(0, 3)
            normalise(0, 1)
            x2(0)
            with dve.Fori(0, NBLK - 1) as i:
                mask_low(i)
                pool_weights(i + 1, 0)
                pool_weights(i + 1, 1)
                x1(i + 1)
                queries_keys(i + 1)
                mask_low2(i)
                score_max(i + 1, 0)
                score_max(i + 1, 1)
                turn(i + 1, 0)
                x3(i)
                score_max(i + 1, 2)
                turn(i + 1, 1)
                score_max(i + 1, 3)
                turn(i + 1, 2)
                normalise(i + 1, 0)
                turn(i + 1, 3)
                normalise(i + 1, 1)
                x2(i + 1)
            mask_low(NBLK - 1)
            mask_low2(NBLK - 1)
            x3(NBLK - 1)


P_E3 = 13
P_COUNT = 19
P_ALL = 40
L0_STEPS = 14


def kernel(**inputs):
    import numpy as np
    import concourse.bacc as bacc
    from concourse.bass_utils import run_bass_kernel_spmd

    a = {k: np.asarray(v) for k, v in inputs.items()}

    def ca(x):
        return np.ascontiguousarray(x)

    def quads(x):
        return np.tile(x, (Q4, 1))

    def by_tile(x):
        return np.repeat(x.reshape(TILES, Q4).T, S, axis=0)

    x = a["x"]
    ints = np.zeros((P, I_END), np.int32)
    ints[:, I_TYPE:I_E2] = by_tile(a["itok_B_0_2"])
    ints[:, I_E2:I_E3] = a["itok_B_0_7"][None, :]
    ints[:, I_E3:I_IDX] = a["itok_B_0_15"][None, :]
    ints[E3, I_E3:I_IDX] = E3 - 1
    ints[:, I_IDX:I_END] = quads(a["itok_Sx32_0_1023"])
    bools = quads(np.concatenate([a["mask_SxS_bk0"], a["mask_Sx32_bk1"]], axis=1)).view(np.int32)
    p = np.arange(P)
    cols = np.zeros((P, C_END), np.float32)
    cols[:, C_SIGN:C_SIGN + S] = np.sign((p % S)[:, None] - np.arange(S)[None, :])
    cols[:, C_IOTA:C_IOTA + S] = np.arange(S)[None, :]
    cols[:, C_U:C_U + TILES] = by_tile(a["condB_uprev"])
    cols[:, C_HEAD:C_HEAD + H4] = ((p % S) // DH)[:, None] == np.arange(H4)[None, :]
    cols[:, C_BQ:C_BQ + HG] = quads(a["L1_cond_bq"].reshape(HG, S).T)
    cols[:, C_BK:C_BK + HG] = quads(a["L1_cond_bk"].reshape(HG, S).T)
    cols[:, C_FC1B:C_FC1B + FC] = a["L3_cond_fc1_b"].reshape(FC, P).T
    cols[:, C_E2] = p // (P // E2)
    cols[:, C_E3] = np.minimum(p, E3 - 1)
    cols[:, C_BO] = a["L1_cond_bo"]
    by_head = lambda w: w.reshape(HG, H4, DH, -1).transpose(1, 0, 2, 3).reshape(D, -1)
    cols[:, C_BV] = by_head(a["L1_cond_bv"])[:, 0]
    cols[0:A0, C_B1] = a["L0_cond_b1"]
    fb3 = np.zeros((E3 + 1, D), np.float32)
    fb3[0:E3, SHARED:] = a["L3_cond_experts_b"]
    fb3[E3, 0:SHARED] = a["L3_cond_fc2_b"]
    chunks = lambda w: w.T.reshape(FC, P, -1).transpose(1, 0, 2)

    arrays = {
        "xt": x.reshape(NBLK, TOK, D).transpose(0, 2, 1),
        "xn": x.reshape(NBLK, G, P, D).transpose(0, 2, 1, 3),
        "ints": ints, "bools": bools, "cols": cols,
        "w1": a["L0_cond_W1"], "vrep": np.repeat(a["L0_cond_v"][:, None], P, axis=1),
        "wq": a["L1_cond_Wq"].T, "wk": a["L1_cond_Wk"].T, "wv": a["L1_cond_Wv"].T,
        "wo": by_head(a["L1_cond_Wo"].T),
        "wit": a["L2_cond_wi"].T, "wot": chunks(a["L2_cond_wo"]),
        "cwia": a["L2_cond_common_wi_a"], "cwibt": a["L2_cond_common_wi_b"].T,
        "cwoa": a["L2_cond_common_wo_a"], "cwobt": a["L2_cond_common_wo_b"].T,
        "ewiat": a["L2_cond_experts_wi_a"].reshape(P, D).T,
        "ewib": a["L2_cond_experts_wi_b"].transpose(0, 2, 1).reshape(P, F),
        "ewoat": chunks(a["L2_cond_experts_wo_a"].reshape(P, F)),
        "ewob": a["L2_cond_experts_wo_b"].transpose(0, 2, 1).reshape(P, D),
        "fc1t": a["L3_cond_fc1_w"].T, "fc2t": chunks(a["L3_cond_fc2_w"]),
        "e3t": a["L3_cond_experts_w"].reshape(E3, PART, FC, P).transpose(3, 0, 2, 1),
        "fb3": fb3, "ident_in": np.eye(P, dtype=np.float32),
    }
    nc = bacc.Bacc("TRN2", target_bir_lowering=False, num_devices=1)
    args = {}
    for name in arrays:
        arrays[name] = ca(arrays[name])
        args[name] = nc.dram_tensor(name + "_dram", arrays[name].shape, mybir.dt.from_np(arrays[name].dtype),
                                    kind="ExternalInput").ap()
    out = nc.dram_tensor("out_dram", (NBLK, P, G, D), F32, kind="ExternalOutput").ap()
    cond_resid_kernel(nc, out=out, **args)
    r = run_bass_kernel_spmd(nc, [{k + "_dram": v for k, v in arrays.items()}], core_ids=[0])
    got = r.results[0]["out_dram"]
    return np.ascontiguousarray(got.transpose(0, 2, 1, 3)).reshape(B, S, D)
```

```python
from contextlib import ExitStack

import concourse.bass as bass
from concourse import mybir

F32 = mybir.dt.float32
F32R = mybir.dt.float32r
I32 = mybir.dt.int32
U8 = mybir.dt.uint8
ALU = mybir.AluOpType
ACT = mybir.ActivationFunctionType
AX = mybir.AxisListType

P = 128
B = 128
S = 32
D = 128
Q4 = P // S
G = 4
TOK = G * P
NBLK = B * S // TOK
ROWS = G * Q4
TILES = B // Q4
A0 = 32
TH = 3
H = 16
DH = D // H
HG = 4
H4 = H // HG
F = 512
FC = F // P
E2 = 8
E3 = 16
PART = 32
SHARED = D - PART
SCALE = DH ** -0.5
NEG = -1e30
LAM_MAX, LAM_RATE, ALPHA = 10.0, 5.0, 2.0

I_TYPE, I_E2, I_E3, I_IDX, I_END = 0, 32, 160, 288, 320
C_SIGN, C_IOTA, C_U, C_HEAD, C_BQ, C_BK, C_FC1B, C_E2, C_E3, C_BO, C_BV, C_B1, C_END = (
    0, 32, 64, 96, 100, 104, 108, 112, 113, 114, 115, 116, 117)


def cond_resid_kernel(nc, xt, xn, ints, bools, cols, w1, vrep, wq, wk, wv, wo, wit, wot, cwia, cwibt,
                      cwoa, cwobt, ewiat, ewib, ewoat, ewob, fc1t, fc2t, e3t, fb3, ident_in, out):
    with ExitStack() as ctx:
        def sb(name, shape, dt=F32):
            return ctx.enter_context(nc.sbuf_tensor(name, shape, dt))

        def bank(name):
            return ctx.enter_context(nc.psum_tensor(name, [P, 512], F32))

        def sem(name):
            return ctx.enter_context(nc.semaphore(name))

        ints_s = sb("ints_s", [P, I_END], I32)
        bools_s = sb("bools_s", [P, 2 * S // 4], I32)
        cols_s = sb("cols_s", [P, C_END])
        w1_s = sb("w1_s", [D, TH * A0])
        vrep_s = sb("vrep_s", [TH * A0, P])
        vpart = sb("vpart", [TH * A0, P], F32R)
        wq_s, wk_s, wv_s, wo_s = (sb(n, [D, D]) for n in ("wq_s", "wk_s", "wv_s", "wo_s"))
        wit_s = sb("wit_s", [D, F])
        wot_s = sb("wot_s", [P, FC, D])
        cwia_s, cwibt_s = sb("cwia_s", [16, D]), sb("cwibt_s", [16, F])
        cwoa_s, cwobt_s = sb("cwoa_s", [16, F]), sb("cwobt_s", [16, D])
        ewiat_s = sb("ewiat_s", [D, P])
        ewib_s = sb("ewib_s", [P, F])
        ewoat_s = sb("ewoat_s", [P, FC, P])
        ewob_s = sb("ewob_s", [P, D])
        fc1t_s = sb("fc1t_s", [D, F])
        e3t_s = sb("e3t_s", [P, E3, FC, PART])
        fb3_s = sb("fb3_s", [E3 + 1, D])
        ident = sb("ident", [P, P])

        def parts(name, shape):
            return sb(name + "_h", shape, F32R), sb(name + "_l", shape, F32R)

        wit_p, ewiat_p, ewib_p, fc1t_p = (parts(n, [P, w]) for n, w in (
            ("wit", F), ("ewiat", P), ("ewib", F), ("fc1t", F)))
        wot_p, ewoat_p = parts("wot", [P, FC, D]), parts("ewoat", [P, FC, P])
        ewob_p = parts("ewob", [P, D])

        intf = sb("intf", [P, I_END])
        neg_c = sb("neg_c", [P, TILES])
        masked = sb("masked", [P, TILES, S])
        cnt = sb("cnt", [P, TILES])
        idxm = sb("idxm", [P, S])
        mk = sb("mk", [P, 2 * S])
        ctab = sb("ctab", [P, S])
        ltab = sb("ltab", [P, S])
        ztab = sb("ztab", [P, S])
        ntab = sb("ntab", [P, S])
        lam = sb("lam", [P, TILES])
        hi = sb("hi", [P, TILES])
        lo = sb("lo", [P, TILES])
        cd = sb("cd", [P, TILES])
        bias = sb("bias", [P, TILES, S])
        hits = bias
        oh2 = sb("oh2", [P, B])
        oh3 = sb("oh3", [E3 + 1, B])
        e3i = sb("e3i", [P, B], I32)
        fbias = sb("fbias", [D, B])
        bo_eff = sb("bo_eff", [D, 1])
        spare = sb("spare", [P, 1])

        xT, xN = sb("xT", [D, TOK]), sb("xN", [P, G, D])
        th = sb("th", [TH * A0, TOK])
        thp = sb("thp", [TH * A0, TOK], F32R)
        l0s = sb("l0s", [P, G, S])
        l0e = sb("l0e", [P, G, S])
        l0m, l0d, l0r = sb("l0m", [P, G]), sb("l0d", [P, G]), sb("l0r", [P, G])
        l0c = sb("l0c", [P, G])
        poolP = sb("poolP", [P, G, P])
        x1T = sb("x1T", [D, TOK])
        qf = sb("qf", [P, TOK])
        qb = sb("qb", [P, HG, G, P])
        kb = sb("kb", [P, HG, H4, G, S])
        vb = sb("vb", [P, G, H, Q4, DH + 1])
        sc = sb("sc", [P, 2, H, S])
        rmax = sb("rmax", [P, 2, H])
        ex = sb("ex", [P, 2, H, S])
        pt = sb("pt", [P, 2, H, S])
        btmp = pt[:, :, :, :].rearrange("p a h s -> p (a h) s")
        rc = sb("rc", [P, 2, HG, Q4])
        on = sb("on", [P, 2, Q4, HG, DH])
        oT = sb("oT", [P, G, P])
        x2T = sb("x2T", [D, TOK])
        x2p = parts("x2", [D, TOK])

        lowm, lowm2 = sb("lowm", [P, TOK]), sb("lowm2", [P, TOK])
        lowp, lowp2 = parts("lowp", [P, TOK]), parts("lowp2", [P, TOK])
        hid = parts("hid", [P, FC, TOK])
        x3T = sb("x3T", [D, TOK])
        x3p = parts("x3", [D, TOK])
        x3b = sb("x3b", [D, TOK])
        x3n = sb("x3n", [P, TOK])
        hT = sb("hT", [P, FC, TOK])
        rw = sb("rw", [P, ROWS, FC, D])
        o_s = sb("o_s", [P, G, D])

        pA0, pA1, pS0, pS1, pV, pB0, pB1, pB2 = (
            bank(n) for n in ("pA0", "pA1", "pS0", "pS1", "pV", "pB0", "pB1", "pB2"))
        pS = [pS0, pS1]
        GIN = [pB1, pB2, pS0, pS1]

        ld_small, ld_attn, ld_ffn, ld_rw = sem("ld_small"), sem("ld_attn"), sem("ld_ffn"), sem("ld_rw")
        ld_xT, ld_xN, st_out = sem("ld_xT"), sem("ld_xN"), sem("st_out")
        prep = sem("prep")
        w_split = sem("w_split")
        prep_act, prep_pe, prep_pool = sem("prep_act"), sem("prep_pe"), sem("prep_pool")
        tables = sem("tables")
        h_ps, th_sb, thl_sb, s_ps = sem("h_ps"), sem("th_sb"), sem("thl_sb"), sem("s_ps")
        l0_step, l0_exp, pool_ps, x1_sb = sem("l0_step"), sem("l0_exp"), sem("pool_ps"), sem("x1_sb")
        q_ps, k_ps, v_ps = sem("q_ps"), sem("k_ps"), sem("v_ps")
        qf_sb, q_sb, k_sb, v_sb = sem("qf_sb"), sem("q_sb"), sem("k_sb"), sem("v_sb")
        sc_ps, sc_sb, mx_sb = sem("sc_ps"), sem("sc_sb"), sem("mx_sb")
        sub_sb, ex_sb, pt_sb, pv_ps = sem("sub_sb"), sem("ex_sb"), sem("pt_sb"), sem("pv_ps")
        rc_sb, on_sb, o_sb = sem("rc_sb"), sem("on_sb"), sem("o_sb")
        wo_ps, x2_sb, x2h_sb, x2l_sb = sem("wo_ps"), sem("x2_sb"), sem("x2h_sb"), sem("x2l_sb")
        low_ps, low_sb, lowl_sb = sem("low_ps"), sem("low_sb"), sem("lowl_sb")
        low2_ps, low2_sb, lowl2_sb = sem("low2_ps"), sem("low2_sb"), sem("lowl2_sb")
        hid_ps, hid_sb, hidl_sb = sem("hid_ps"), sem("hid_sb"), sem("hidl_sb")
        out_ps, x3_sb, x3b_sb = sem("out_ps"), sem("x3_sb"), sem("x3b_sb")
        x3l_sb, x3t_ps, x3n_sb = sem("x3l_sb"), sem("x3t_ps"), sem("x3n_sb")
        g_ps, g_sb = sem("g_ps"), sem("g_sb")
        rw_sb, fin_ps, res_sb = sem("rw_sb"), sem("fin_ps"), sem("res_sb")

        def at(eng, s, value):
            if isinstance(value, int) and value <= 0:
                return
            eng.wait_ge(s, value)

        N_SMALL, N_ATTN, N_FFN = 3, 6, 13
        PREP_VEC, SPLITS = [0], [0]

        block = ctx.enter_context(nc.Block())

        @block.sync
        def _(sp):
            sp.dma_start(ints_s[:, :], ints).then_inc(ld_small, 16)
            sp.dma_start(bools_s[:, :], bools).then_inc(ld_small, 16)
            sp.dma_start(cols_s[:, :], cols).then_inc(ld_small, 16)

            def load_x(i):
                at(sp, x1_sb, i)
                sp.dma_start(xT[:, :], xt[i]).then_inc(ld_xT, 16)
                at(sp, pool_ps, i)
                sp.dma_start(xN[:, :, :], xn[i]).then_inc(ld_xN, 16)

            def store(i):
                at(sp, res_sb, i + 1)
                sp.dma_start(out[i], o_s[:, :, :]).then_inc(st_out, 16)

            sp.sem_inc(st_out, 16)
            load_x(0)
            for dst, src in ((w1_s, w1), (vrep_s, vrep), (wq_s, wq), (wk_s, wk), (wv_s, wv), (wo_s, wo)):
                sp.dma_start(dst[:, :], src).then_inc(ld_attn, 16)
            for dst, src in ((cwia_s[:, :], cwia), (cwibt_s[:, :], cwibt), (cwoa_s[:, :], cwoa),
                             (cwobt_s[:, :], cwobt), (fb3_s[:, :], fb3), (ident[:, :], ident_in),
                             (wit_s[:, :], wit), (wot_s[:, :, :], wot),
                             (ewiat_s[:, :], ewiat), (ewib_s[:, :], ewib), (ewoat_s[:, :, :], ewoat),
                             (ewob_s[:, :], ewob), (fc1t_s[:, :], fc1t)):
                sp.dma_start(dst, src).then_inc(ld_ffn, 16)
            sp.dma_start(e3t_s[:, :, :, :], e3t).then_inc(ld_rw, 16)
            for r in range(ROWS):
                sp.dma_start(rw[:, r, :, 0:SHARED], fc2t).then_inc(ld_rw, 16)
            load_x(1)
            load_x(2)
            with sp.Fori(3, NBLK) as n:
                load_x(n)
                store(n - 3)
            store(NBLK - 3)
            store(NBLK - 2)
            store(NBLK - 1)
            sp.wait_ge(st_out, 16 * (NBLK + 1))

        @block.gpsimd
        def _(pool):
            pool.memset(poolP[:, :, :], 0.0).then_inc(prep_pool, 1)
            pool.memset(qb[:, :, :, :], 0.0).then_inc(prep_pool, 1)
            pool.memset(vb[:, :, :, :, :], 0.0).then_inc(prep_pool, 1)
            pool.wait_ge(prep_pool, 3)
            for q in range(Q4):
                pool.memset(vb[S * q:S * q + S, :, :, q, DH:DH + 1], 1.0).then_inc(prep_pool, 1)

            def subtract_max(i, g):
                at(pool, mx_sb, G * i + g + 1)
                pool.tensor_tensor(sc[:, g % 2, :, :], sc[:, g % 2, :, :],
                                   rmax[:, g % 2, :].unsqueeze(2).to_broadcast([P, H, S]),
                                   ALU.subtract).then_inc(sub_sb, 1)

            def queries(i):
                at(pool, qf_sb, i + 1)
                for q in range(Q4):
                    k = slice(S * q, S * q + S)
                    pool.tensor_tensor(
                        qb[k, :, :, k], qf[k, :].rearrange("p (a g s) -> p a g s", a=HG, g=G),
                        cols_s[k, C_BQ:C_BQ + HG].unsqueeze(2).unsqueeze(3).to_broadcast([S, HG, G, S]),
                        ALU.add).then_inc(q_sb, 1)
                at(pool, q_sb, Q4 * (i + 1))

            def biased_x3(i):
                at(pool, x3_sb, 2 * i + 1)
                at(pool, x3t_ps, i)
                pool.tensor_tensor(x3b[:, :].rearrange("p (r s) -> p r s", s=S),
                                   x3T[:, :].rearrange("p (r s) -> p r s", s=S),
                                   fbias[:, bass.ds(ROWS * i, ROWS)].unsqueeze(2).to_broadcast([P, ROWS, S]),
                                   ALU.add).then_inc(x3b_sb, 1)

            def expert_weights(i, part):
                if part == 0:
                    at(pool, fin_ps, i + 1)
                for r in range(Q4 * part, Q4 * part + Q4):
                    e = pool.value_load(e3i[0:1, bass.ds(ROWS * i + r, 1)], min_val=0, max_val=E3 - 1)
                    pool.tensor_copy(rw[:, r, :, SHARED:D],
                                     e3t_s[:, bass.ds(e, 1), :, :].rearrange("p o c n -> p (o c) n"))\
                        .then_inc(rw_sb, 1)

            def split(whole, pair):
                pool.tensor_copy(pair[0], whole).then_inc(w_split, 1)
                SPLITS[0] += 1
                pool.wait_ge(w_split, SPLITS[0])
                pool.tensor_tensor(pair[1], whole, pair[0], ALU.subtract).then_inc(w_split, 1)
                SPLITS[0] += 1

            pool.wait_ge(prep_pool, 3 + Q4)
            pool.wait_ge(ld_ffn, 16 * N_FFN)
            queries(0)
            for whole, pair in ((ewiat_s, ewiat_p), (ewib_s, ewib_p), (ewob_s, ewob_p), (fc1t_s, fc1t_p)):
                split(whole[:, :], [x[:, :] for x in pair])
            split(ewoat_s[:, :, :], [x[:, :, :] for x in ewoat_p])
            pool.wait_ge(prep, P_ALL)
            for g in range(2):
                subtract_max(0, g)
            split(wit_s[:, :], [x[:, :] for x in wit_p])
            for g in range(2, G):
                subtract_max(0, g)
            split(wot_s[:, :, :], [x[:, :, :] for x in wot_p])

            def step_of(n):
                at(pool, x3b_sb, n - 1)
                if isinstance(n, int) and n == 1:
                    at(pool, w_split, SPLITS[0])
                queries(n)
                if isinstance(n, int) and n == 1:
                    pool.wait_ge(ld_rw, 16 * (1 + ROWS))
                subtract_max(n, 0)
                subtract_max(n, 1)
                expert_weights(n - 1, 0)
                subtract_max(n, 2)
                expert_weights(n - 1, 1)
                subtract_max(n, 3)
                expert_weights(n - 1, 2)
                expert_weights(n - 1, 3)
                biased_x3(n - 1)

            step_of(1)
            with pool.Fori(2, NBLK) as n:
                step_of(n)
            for part in range(G):
                expert_weights(NBLK - 1, part)
            biased_x3(NBLK - 1)

        @block.scalar
        def _(act):
            act.wait_ge(ld_small, 16 * N_SMALL)
            act.activation(lam[:, :], cols_s[:, C_U:C_U + TILES], ACT.Exp, scale=-LAM_RATE).then_inc(prep_act, 1)

            def tanh(i):
                at(act, h_ps, i + 1)
                for dst in (thp, th):
                    act.activation(dst[:, :], pA0[0:TH * A0, :], ACT.Tanh,
                                   bias=cols_s[0:TH * A0, C_B1:C_B1 + 1]).then_inc(th_sb, 1)

            def l0_exps(i):
                at(act, l0_step, L0_STEPS * i + 6)
                act.activation(l0e[:, :, :], l0s[:, :, :], ACT.Exp).then_inc(l0_exp, 1)

            def queries(i):
                at(act, q_ps, i + 1)
                at(act, q_sb, Q4 * i)
                act.activation(qf[:, :], pA1[:, :], ACT.Copy).then_inc(qf_sb, 1)

            def values(i):
                at(act, v_ps, i + 1)
                for q in range(Q4):
                    part = slice(S * q, S * q + S)
                    act.activation(vb[part, :, :, q, 0:DH].rearrange("p g h d -> p (g h) d"),
                                   pV[part, :].rearrange("p (n d) -> p n d", d=DH), ACT.Copy).then_inc(v_sb, 1)

            def exps(i, g):
                t = G * i + g
                at(act, sub_sb, t + 1)
                at(act, pt_sb, t - 1)
                act.activation(ex[:, g % 2, :, :], sc[:, g % 2, :, :], ACT.Exp).then_inc(ex_sb, 1)

            def relu(i, c):
                at(act, hid_ps, FC * i + c + 1)
                act.activation(hid[0][:, c, :], [pB1, pB2, pB0, pB1][c][:, :], ACT.Relu).then_inc(hid_sb, 1)

            def gelu(i, c):
                at(act, g_ps, FC * i + c + 1)
                act.activation(hT[:, c, :], GIN[c][:, :], ACT.Gelu,
                               bias=cols_s[:, C_FC1B + c:C_FC1B + c + 1]).then_inc(g_sb, 1)

            def x2_high(i):
                at(act, x2_sb, i + 1)
                act.activation(x2p[0][:, :], x2T[:, :], ACT.Copy).then_inc(x2h_sb, 1)

            def table(n, function):
                at(act, tables, 2 * n - (2 if function is ACT.Exp else 1))
                act.activation(spare[:, :], cols_s[:, C_IOTA:C_IOTA + 1], function).then_inc(tables, 1)

            def token_major(i):
                at(act, x3t_ps, i + 1)
                act.activation(x3n[:, :], pB0[:, :], ACT.Copy).then_inc(x3n_sb, 1)

            act.wait_ge(prep_pool, 3 + Q4)
            tanh(0)
            l0_exps(0)
            queries(0)
            act.wait_ge(prep, P_COUNT)
            act.activation(ltab[:, :], ctab[:, :], ACT.Ln).then_inc(prep_act, 1)
            values(0)
            for g in range(G):
                exps(0, g)
            tanh(1)
            l0_exps(1)
            x2_high(0)

            def step_of(n, last, next_block=True):
                queries(n)
                table(n, ACT.Exp)
                if last is not None:
                    token_major(last)
                exps(n, 0)
                values(n)
                relu(n - 1, 0)
                exps(n, 1)
                relu(n - 1, 1)
                exps(n, 2)
                if next_block:
                    tanh(n + 1)
                relu(n - 1, 2)
                relu(n - 1, 3)
                exps(n, 3)
                if next_block:
                    l0_exps(n + 1)
                table(n, ACT.Gelu)
                x2_high(n)
                for c in range(FC):
                    gelu(n - 1, c)

            step_of(1, None)
            with act.Fori(2, NBLK - 1) as n:
                step_of(n, n - 2)
            step_of(NBLK - 1, NBLK - 3, False)
            token_major(NBLK - 2)
            for c in range(FC):
                relu(NBLK - 1, c)
            for c in range(FC):
                gelu(NBLK - 1, c)
            token_major(NBLK - 1)

        @block.tensor
        def _(pe):
            mm = pe.matmul

            def scorer_in(i):
                at(pe, ld_xT, 16 * (i + 1))
                at(pe, k_sb, HG * i)
                mm(pA0[0:TH * A0, :], w1_s[:, :], xT[:, :], start=True, stop=True).then_inc(h_ps, 1)

            def scorer_out(i):
                at(pe, thl_sb, i + 1)
                at(pe, qf_sb, i)
                mm(pA1[:, :], vpart[:, :], thp[:, :], start=True, stop=True).then_inc(s_ps, 1)

            def pooling(i):
                at(pe, ld_xN, 16 * (i + 1))
                at(pe, l0_step, L0_STEPS * (i + 1))
                for g in range(G):
                    last = mm(pA0[:, P * g:P * g + P], xN[:, g, :], poolP[:, g, :], start=True, stop=True)
                last.then_inc(pool_ps, 1)

            def project(i, ps, w, done):
                at(pe, x1_sb, i + 1)
                rows = x1T[:, :].rearrange("p (g q s) -> p g q s", g=G, q=Q4)
                for hg in range(HG):
                    for q in range(Q4):
                        last = mm(ps[S * q:S * q + S, P * hg:P * hg + P], w[:, S * hg:S * hg + S],
                                  rows[:, :, q, :], start=True, stop=True)
                last.then_inc(done, 1)

            def queries(i):
                project(i, pA1, wq_s, q_ps)

            def keys(i):
                project(i, pA0, wk_s, k_ps)

            def values(i):
                at(pe, x2_sb, i)
                for g in range(G):
                    last = mm(pV[:, P * g:P * g + P], x1T[:, P * g:P * g + P], wv_s[:, :], start=True, stop=True)
                last.then_inc(v_ps, 1)

            def scores(i, g):
                if g == 0:
                    at(pe, q_sb, Q4 * (i + 1))
                    at(pe, k_sb, HG * (i + 1))
                    at(pe, g_sb, FC * (i - 1))
                at(pe, sc_sb, G * i + g - 1)
                for hg in range(HG):
                    last = mm(pS[g % 2][:, P * hg:P * hg + P], qb[:, hg, g, :], kb[:, hg, :, g, :],
                              start=True, stop=True)
                last.then_inc(sc_ps, 1)

            def weigh(i, g):
                at(pe, pt_sb, G * i + g + 1)
                if g == 0:
                    at(pe, v_sb, Q4 * (i + 1))
                if g == 2:
                    at(pe, on_sb, G * i + 2)
                w = Q4 * (DH + 1)
                for hg in range(HG):
                    for h4 in range(H4):
                        h = H4 * hg + h4
                        at_col = (g % 2) * HG * w + hg * w
                        last = mm(pV[S * h4:S * h4 + S, at_col:at_col + w], pt[:, g % 2, h, :],
                                  vb[:, g, h, :, :], start=True, stop=True)
                last.then_inc(pv_ps, 1)

            def attn_out(i):
                at(pe, o_sb, G // 2 * (i + 1))
                mm(pV[:, :], wo_s[:, :], oT[:, :, :], start=True, stop=True).then_inc(wo_ps, 1)

            def parts3(ps, w, x, start, stop):
                mm(ps, w[0], x[0], start=start, stop=False)
                mm(ps, w[0], x[1], start=False, stop=False)
                return mm(ps, w[1], x[0], start=False, stop=stop)

            def cols_of(pair, c):
                return [w[:, P * c:P * c + P] for w in pair]

            def chunk(pair, c):
                return [w[:, c, :] for w in pair]

            def whole(pair):
                return [w[:, :] for w in pair]

            HID = [pB1, pB2, pB0, pB1]

            def low(i):
                at(pe, x2h_sb, i + 1)
                at(pe, x2l_sb, i + 1)
                at(pe, x3_sb, 2 * i - 1)
                parts3(pB0[:, :], whole(ewiat_p), whole(x2p), True, True).then_inc(low_ps, 1)

            def hidden(i, c):
                if c == 1:
                    at(pe, res_sb, i)
                if c == 2:
                    at(pe, x3n_sb, i)
                if c == 3:
                    at(pe, hidl_sb, FC * i + 1)
                parts3(HID[c][:, :], cols_of(wit_p, c), whole(x2p), True, False)

            def hidden_expert(i, c):
                at(pe, low_sb, 2 * (i + 1))
                at(pe, lowl_sb, i + 1)
                parts3(HID[c][:, :], cols_of(ewib_p, c), whole(lowp), False, True).then_inc(hid_ps, 1)

            def low2(i):
                at(pe, hidl_sb, FC * i + 2)
                for c in range(FC):
                    at(pe, hidl_sb, FC * i + c + 1)
                    last = parts3(pB2[:, :], chunk(ewoat_p, c), chunk(hid, c), c == 0, c == FC - 1)
                last.then_inc(low2_ps, 1)

            def out2(i):
                for c in range(FC):
                    parts3(pB0[:, :], chunk(wot_p, c), chunk(hid, c), c == 0, False)

            def out2_expert(i):
                at(pe, lowl2_sb, i + 1)
                parts3(pB0[:, :], whole(ewob_p), whole(lowp2), False, True).then_inc(out_ps, 1)

            def fc1(i, c):
                if c == 0:
                    at(pe, x3l_sb, i + 1)
                if c == 2:
                    at(pe, sc_sb, G * NBLK if isinstance(i, int) and i == NBLK - 1 else G * (i + 2))
                parts3(GIN[c][:, :], cols_of(fc1t_p, c), whole(x3p), True, True)\
                    .then_inc(g_ps, 1)

            def token_major(i):
                at(pe, x3b_sb, i + 1)
                at(pe, low_sb, 2 * NBLK if isinstance(i, int) and i == NBLK - 1 else 2 * (i + 2) - 1)
                for g in range(G):
                    last = pe.transpose(pB0[:, P * g:P * g + P], x3b[:, P * g:P * g + P], ident[:, :])
                last.then_inc(x3t_ps, 1)

            def final(i, g):
                if g == 0:
                    at(pe, rw_sb, ROWS * (i + 1))
                    at(pe, g_sb, FC * (i + 1))
                for c in range(FC):
                    for q in range(Q4):
                        tok = slice(P * g + S * q, P * g + S * q + S)
                        last = mm(pB2[S * q:S * q + S, P * g:P * g + P], hT[:, c, tok],
                                  rw[:, Q4 * g + q, c, :], start=(c == 0), stop=(c == FC - 1))
                if g == G - 1:
                    last.then_inc(fin_ps, 1)

            def prepare():
                pe.wait_ge(ld_ffn, 16 * N_FFN)
                mm(pB0[:, :], cwia_s[:, :], cwibt_s[:, :], start=True, stop=True).then_inc(prep_pe, 1)
                for c in range(FC):
                    last = mm(pB1[:, P * c:P * c + P], cwoa_s[:, P * c:P * c + P], cwobt_s[:, :], start=True, stop=True)
                last.then_inc(prep_pe, 1)
                mm(pB2[:, 0:1], wo_s[:, :], cols_s[:, C_BV:C_BV + 1], start=True, stop=True).then_inc(prep_pe, 1)
                pe.wait_ge(prep, P_E3)
                mm(pB2[:, P:P + B], fb3_s[:, :], oh3[:, :], start=True, stop=True).then_inc(prep_pe, 1)

            pe.wait_ge(ld_small, 16 * N_SMALL)
            pe.wait_ge(ld_attn, 16 * N_ATTN)
            pe.sem_inc(fin_ps, 1)
            scorer_in(0)
            scorer_out(0)
            pe.wait_ge(prep_pool, 3 + Q4)
            pooling(0)
            queries(0)
            keys(0)
            values(0)
            prepare()
            scores(0, 0)
            scores(0, 1)
            weigh(0, 0)
            scores(0, 2)
            weigh(0, 1)
            scores(0, 3)
            scorer_in(1)
            weigh(0, 2)
            scorer_out(1)
            weigh(0, 3)
            attn_out(0)
            pooling(1)

            def step_of(n, last, next_block=True):
                if last is None:
                    pe.wait_ge(w_split, 2 * 7)
                low(n - 1)
                queries(n)
                keys(n)
                if last is not None:
                    token_major(last)
                    final(last, 0)
                    final(last, 1)
                if last is not None:
                    final(last, 2)
                scores(n, 0)
                scores(n, 1)
                if last is not None:
                    final(last, 3)
                values(n)
                hidden(n - 1, 0)
                hidden_expert(n - 1, 0)
                scores(n, 2)
                hidden(n - 1, 1)
                hidden_expert(n - 1, 1)
                weigh(n, 0)
                if next_block:
                    scorer_in(n + 1)
                scores(n, 3)
                hidden(n - 1, 2)
                hidden_expert(n - 1, 2)
                weigh(n, 1)
                hidden(n - 1, 3)
                hidden_expert(n - 1, 3)
                if next_block:
                    scorer_out(n + 1)
                weigh(n, 2)
                low2(n - 1)
                weigh(n, 3)
                out2(n - 1)
                out2_expert(n - 1)
                if next_block:
                    pooling(n + 1)
                attn_out(n)
                for c in range(FC):
                    fc1(n - 1, c)

            step_of(1, None)
            with pe.Fori(2, NBLK - 1) as n:
                step_of(n, n - 2)
            step_of(NBLK - 1, NBLK - 3, False)
            low(NBLK - 1)
            token_major(NBLK - 2)
            for g in range(G):
                final(NBLK - 2, g)
            for c in range(FC):
                hidden(NBLK - 1, c)
                hidden_expert(NBLK - 1, c)
            low2(NBLK - 1)
            out2(NBLK - 1)
            out2_expert(NBLK - 1)
            for c in range(FC):
                fc1(NBLK - 1, c)
            token_major(NBLK - 1)
            for g in range(G):
                final(NBLK - 1, g)

        @block.vector
        def _(dve):
            tt, ts, stt = dve.tensor_tensor, dve.tensor_scalar, dve.scalar_tensor_tensor

            def step(ins):
                PREP_VEC[0] += 1
                ins.then_inc(prep, 1)
                dve.wait_ge(prep, PREP_VEC[0])

            def wrap(col, width, n):
                x, t = intf[:, col:col + width], btmp[:, 0:4, :].rearrange("p a b -> p (a b)")[:, 0:width]
                step(ts(t, x, 0.0, float(n), ALU.is_lt, ALU.mult))
                step(tt(x, x, t, ALU.add))
                step(ts(x, x, 0.0, float(n - 1), ALU.max, ALU.min))

            def prepare_pooling():
                dve.wait_ge(ld_small, 16 * N_SMALL)
                step(dve.tensor_copy(intf[:, :], ints_s[:, :]))
                step(ts(cnt[:, :], intf[:, I_TYPE:I_TYPE + TILES], 0.0, None, ALU.is_equal))
                step(stt(neg_c[:, :], intf[:, I_TYPE:I_TYPE + TILES], 1.0, cnt[:, :], ALU.is_equal, ALU.subtract))
                step(tt(masked[:, :, :], cols_s[:, C_SIGN:C_SIGN + S].unsqueeze(1).to_broadcast([P, TILES, S]),
                        neg_c[:, :].unsqueeze(2).to_broadcast([P, TILES, S]), ALU.is_equal))
                step(dve.tensor_reduce(cnt[:, :], masked[:, :, :], AX.X, ALU.add))
                step(ts(cnt[:, :], cnt[:, :], -1.0, float(S), ALU.mult, ALU.add))
                dve.wait_ge(ld_attn, 16 * N_ATTN)
                two = 2 * A0
                step(dve.tensor_copy(vpart[:, :], vrep_s[:, :]))
                step(tt(vpart[two:, :], vrep_s[two:, :], vpart[two:, :], ALU.subtract))
                dve.wait_ge(prep_pool, 3 + Q4)

            def prepare_ids():
                step(dve.tensor_copy(mk[:, :], bools_s[:, :].bitcast(U8)))
                wrap(I_IDX, S, S)
                wrap(I_E2, B, E2)
                wrap(I_E3, B, E3)
                step(dve.tensor_copy(e3i[:, :], intf[:, I_E3:I_E3 + B]))
                step(ts(oh3[:, :], intf[0:E3 + 1, I_E3:I_E3 + B], cols_s[0:E3 + 1, C_E3:C_E3 + 1], None, ALU.is_equal))
                assert PREP_VEC[0] == P_E3
                step(ts(oh2[:, :], intf[:, I_E2:I_E2 + B], cols_s[:, C_E2:C_E2 + 1], ALPHA, ALU.is_equal, ALU.mult))

            def prepare_counts():
                step(stt(idxm[:, :], intf[:, I_IDX:I_IDX + S], 1.0, mk[:, S:2 * S], ALU.add, ALU.mult))
                step(ts(idxm[:, :], idxm[:, :], -1.0, None, ALU.add))
                step(tt(hits[:, :, :], idxm[:, :].unsqueeze(1).to_broadcast([P, S, S]),
                        cols_s[:, C_IOTA:C_IOTA + S].unsqueeze(2).to_broadcast([P, S, S]), ALU.is_equal))
                step(dve.tensor_reduce(ntab[:, :], hits[:, :, :], AX.X, ALU.add))
                step(ts(ctab[:, :], ntab[:, :], 1.0, None, ALU.max))
                assert PREP_VEC[0] == P_COUNT
                step(ts(ztab[:, :], ntab[:, :], -0.5, -2 * NEG, ALU.add, ALU.mult))
                step(ts(ntab[:, :], mk[:, 0:S], -1.0, 1.0, ALU.mult, ALU.add))
                dve.wait_ge(prep_act, 1)
                step(ts(lam[:, :], lam[:, :], LAM_MAX, None, ALU.mult))
                step(ts(hi[:, :], lam[:, :], 1.0, -2 * NEG, ALU.is_ge, ALU.mult))
                step(ts(lo[:, :], hi[:, :], -1.0, None, ALU.mult))
                step(stt(cd[:, :], lam[:, :], 1.0, lam[:, :], ALU.is_lt, ALU.mult))
                step(ts(cd[:, :], cd[:, :], -1.0, None, ALU.mult))

            def by_token(x):
                return x[:, :].unsqueeze(1).to_broadcast([P, TILES, S])

            def by_tile(x):
                return x[:, :].unsqueeze(2).to_broadcast([P, TILES, S])

            def prepare_bias():
                dve.wait_ge(prep_act, 2)
                step(tt(ltab[:, :], ltab[:, :], ztab[:, :], ALU.min))
                step(tt(bias[:, :, :], by_token(ltab), by_tile(lo), ALU.max))
                step(tt(bias[:, :, :], bias[:, :, :], by_tile(hi), ALU.min))
                step(tt(btmp[:, :, :], by_token(ntab), by_tile(cd), ALU.mult))
                step(tt(bias[:, :, :], bias[:, :, :], btmp[:, :, :], ALU.add))

            def prepare_products():
                dve.wait_ge(prep_pe, 4)
                step(stt(wit_s[:, :], pB0[:, :], ALPHA, wit_s[:, :], ALU.mult, ALU.add))
                wot_f = wot_s[:, :, :].rearrange("p c d -> p (c d)")
                step(stt(wot_f, pB1[:, :], ALPHA, wot_f, ALU.mult, ALU.add))
                step(tt(bo_eff[:, :], pB2[:, 0:1], cols_s[:, C_BO:C_BO + 1], ALU.add))
                step(dve.tensor_copy(fbias[:, :], pB2[:, P:P + B]))
                assert PREP_VEC[0] == P_ALL

            def scorer_low(i):
                at(dve, th_sb, 2 * (i + 1))
                tt(thp[A0:2 * A0, :], th[A0:2 * A0, :], thp[A0:2 * A0, :], ALU.subtract).then_inc(thl_sb, 1)

            def pool_weights(i, part):
                n = L0_STEPS * i
                if part == 0:
                    at(dve, s_ps, i + 1)
                    tok = pA1[:, :].rearrange("p (g q l) -> p g q l", g=G, q=Q4)
                    for q in range(Q4):
                        k = slice(S * q, S * q + S)
                        stt(l0s[k, :, :], masked[k, bass.ds(G * i, G), :], NEG, tok[k, :, q, :],
                            ALU.mult, ALU.add).then_inc(l0_step, 1)
                    at(dve, l0_step, n + 4)
                    dve.tensor_reduce(l0m[:, :], l0s[:, :, :], AX.X, ALU.max).then_inc(l0_step, 1)
                    at(dve, l0_step, n + 5)
                    tt(l0s[:, :, :], l0s[:, :, :], l0m[:, :].unsqueeze(2).to_broadcast([P, G, S]),
                       ALU.subtract).then_inc(l0_step, 1)
                    return
                at(dve, l0_exp, i + 1)
                dve.tensor_reduce(l0d[:, :], l0e[:, :, :], AX.X, ALU.add).then_inc(l0_step, 1)
                at(dve, l0_step, n + 7)
                tt(l0r[:, :], l0d[:, :], cnt[:, bass.ds(G * i, G)], ALU.mult).then_inc(l0_step, 1)
                at(dve, l0_step, n + 8)
                dve.reciprocal(l0c[:, :], l0r[:, :]).then_inc(l0_step, 1)
                at(dve, l0_step, n + 9)
                tt(l0e[:, :, :], l0e[:, :, :], l0c[:, :].unsqueeze(2).to_broadcast([P, G, S]),
                   ALU.mult).then_inc(l0_step, 1)
                at(dve, l0_step, n + 10)
                for q in range(Q4):
                    k = slice(S * q, S * q + S)
                    dve.transpose(poolP[k, :, k], l0e[k, :, :]).then_inc(l0_step, 1)

            def x1(i):
                at(dve, pool_ps, i + 1)
                at(dve, x2_sb, i)
                tt(x1T[:, :], pA0[:, :], xT[:, :], ALU.add).then_inc(x1_sb, 1)

            def keys(i):
                at(dve, k_ps, i + 1)
                for hg in range(HG):
                    stt(kb[:, hg, :, :, :].rearrange("p h g t -> p h (g t)"),
                        pA0[:, P * hg:P * hg + P].unsqueeze(1).to_broadcast([P, H4, P]),
                        cols_s[:, C_BK + hg:C_BK + hg + 1],
                        cols_s[:, C_HEAD:C_HEAD + H4].unsqueeze(2).to_broadcast([P, H4, P]),
                        ALU.add, ALU.mult).then_inc(k_sb, 1)

            def score_max(i, g):
                t = G * i + g
                at(dve, sc_ps, t + 1)
                at(dve, ex_sb, t - 1)
                stt(sc[:, g % 2, :, :], pS[g % 2][:, :].rearrange("p (h t) -> p h t", t=S), SCALE,
                    bias[:, bass.ds(t, 1), :].to_broadcast([P, H, S]), ALU.mult, ALU.add).then_inc(sc_sb, 1)
                at(dve, sc_sb, t + 1)
                dve.tensor_reduce(rmax[:, g % 2, :], sc[:, g % 2, :, :], AX.X, ALU.max).then_inc(mx_sb, 1)

            def turn(i, g):
                t = G * i + g
                at(dve, ex_sb, t + 1)
                at(dve, pv_ps, t - 1)
                dve.transpose(pt[:, g % 2, :, :], ex[:, g % 2, :, :]).then_inc(pt_sb, 1)

            def normalise(i, pair):
                n = G // 2 * i + pair
                at(dve, pv_ps, 2 * n + 2)
                sums = pV[:, 0:2 * H * (DH + 1)].rearrange("p (n d) -> p n d", d=DH + 1)
                dve.reciprocal(rc[:, :, :, :].rearrange("p t a q -> p (t a q)"), sums[:, :, DH]).then_inc(rc_sb, 1)
                at(dve, rc_sb, n + 1)
                for t in range(2):
                    tt(on[:, t, :, :, :].rearrange("p q a d -> p a q d"),
                       sums[:, H * t:H * t + H, 0:DH].rearrange("p (a q) d -> p a q d", q=Q4),
                       rc[:, t, :, :].unsqueeze(3).to_broadcast([P, HG, Q4, DH]), ALU.mult).then_inc(on_sb, 1)
                at(dve, on_sb, 2 * n + 2)
                dve.transpose(oT[:, 2 * pair:2 * pair + 2, :],
                              on[:, :, :, :, :].rearrange("p t q a d -> p t (q a d)")).then_inc(o_sb, 1)

            def x2(i):
                at(dve, wo_ps, i + 1)
                stt(x2T[:, :], pV[:, :], bo_eff[:, 0:1], x1T[:, :], ALU.add, ALU.add).then_inc(x2_sb, 1)

            def x2_low(i):
                at(dve, x2h_sb, i + 1)
                tt(x2p[1][:, :], x2T[:, :], x2p[0][:, :], ALU.subtract).then_inc(x2l_sb, 1)

            def rows_of(x, i):
                return x[:, bass.ds(ROWS * i, ROWS)].unsqueeze(2).to_broadcast([P, ROWS, S])

            def by_row(x):
                return x[:, :].rearrange("p (r s) -> p r s", s=S)

            def mask_low(i, ps=None, whole=None, pair=None, seen=None, done=None, low_done=None):
                ps, whole, pair, seen, done, low_done = (
                    ps or pB0, whole or lowm, pair or lowp, seen or low_ps, done or low_sb, low_done or lowl_sb)
                at(dve, seen, i + 1)
                tt(by_row(whole), by_row(ps), rows_of(oh2, i), ALU.mult).then_inc(done, 1)
                at(dve, done, 2 * i + 1)
                dve.tensor_copy(pair[0][:, :], whole[:, :]).then_inc(done, 1)
                at(dve, done, 2 * i + 2)
                tt(pair[1][:, :], whole[:, :], pair[0][:, :], ALU.subtract).then_inc(low_done, 1)

            def mask_low2(i):
                mask_low(i, pB2, lowm2, lowp2, low2_ps, low2_sb, lowl2_sb)

            def relu_low(i, c):
                at(dve, hid_sb, FC * i + c + 1)
                stt(hid[1][:, c, :], [pB1, pB2, pB0, pB1][c][:, :], 0.0, hid[0][:, c, :],
                    ALU.max, ALU.subtract).then_inc(hidl_sb, 1)

            def x3(i):
                at(dve, out_ps, i + 1)
                tt(x3T[:, :], pB0[:, :], x2T[:, :], ALU.add).then_inc(x3_sb, 1)
                at(dve, x3_sb, 2 * i + 1)
                dve.tensor_copy(x3p[0][:, :], x3T[:, :]).then_inc(x3_sb, 1)
                at(dve, x3_sb, 2 * i + 2)
                tt(x3p[1][:, :], x3T[:, :], x3p[0][:, :], ALU.subtract).then_inc(x3l_sb, 1)

            def result(i):
                at(dve, fin_ps, i + 2)
                at(dve, x3n_sb, i + 1)
                at(dve, st_out, 16 * (i + 1))
                tt(o_s[:, :, :].rearrange("p g d -> p (g d)"), pB2[:, :], x3n[:, :], ALU.add).then_inc(res_sb, 1)

            prepare_pooling()
            scorer_low(0)
            pool_weights(0, 0)
            prepare_ids()
            pool_weights(0, 1)
            x1(0)
            prepare_counts()
            keys(0)
            prepare_bias()
            prepare_products()
            score_max(0, 0)
            score_max(0, 1)
            turn(0, 0)
            score_max(0, 2)
            turn(0, 1)
            score_max(0, 3)
            turn(0, 2)
            normalise(0, 0)
            turn(0, 3)
            scorer_low(1)
            normalise(0, 1)
            pool_weights(1, 0)
            pool_weights(1, 1)
            x2(0)
            x1(1)

            def step_of(n, last, next_block=True):
                x2_low(n - 1)
                mask_low(n - 1)
                keys(n)
                score_max(n, 0)
                score_max(n, 1)
                if last is not None:
                    result(last)
                turn(n, 0)
                score_max(n, 2)
                relu_low(n - 1, 0)
                turn(n, 1)
                relu_low(n - 1, 1)
                score_max(n, 3)
                if next_block:
                    scorer_low(n + 1)
                turn(n, 2)
                normalise(n, 0)
                relu_low(n - 1, 2)
                relu_low(n - 1, 3)
                if next_block:
                    pool_weights(n + 1, 0)
                turn(n, 3)
                if next_block:
                    pool_weights(n + 1, 1)
                mask_low2(n - 1)
                normalise(n, 1)
                x3(n - 1)
                x2(n)
                if next_block:
                    x1(n + 1)

            step_of(1, None)
            with dve.Fori(2, NBLK - 1) as n:
                step_of(n, n - 2)
            step_of(NBLK - 1, NBLK - 3, False)
            x2_low(NBLK - 1)
            mask_low(NBLK - 1)
            result(NBLK - 2)
            for c in range(FC):
                relu_low(NBLK - 1, c)
            mask_low2(NBLK - 1)
            x3(NBLK - 1)
            result(NBLK - 1)


P_E3 = 20
P_COUNT = 26
P_ALL = 42
L0_STEPS = 14


def kernel(**inputs):
    import numpy as np
    import concourse.bacc as bacc
    from concourse.bass_utils import run_bass_kernel_spmd

    a = {k: np.asarray(v) for k, v in inputs.items()}

    def ca(x):
        return np.ascontiguousarray(x)

    def quads(x):
        return np.tile(x, (Q4, 1))

    def by_tile(x):
        return np.repeat(x.reshape(TILES, Q4).T, S, axis=0)

    x = a["x"]
    ints = np.zeros((P, I_END), np.int32)
    ints[:, I_TYPE:I_E2] = by_tile(a["itok_B_0_2"])
    ints[:, I_E2:I_E3] = a["itok_B_0_7"][None, :]
    ints[:, I_E3:I_IDX] = a["itok_B_0_15"][None, :]
    ints[E3, I_E3:I_IDX] = E3 - 1
    ints[:, I_IDX:I_END] = quads(a["itok_Sx32_0_1023"])
    bools = quads(np.concatenate([a["mask_SxS_bk0"], a["mask_Sx32_bk1"]], axis=1)).view(np.int32)
    p = np.arange(P)
    cols = np.zeros((P, C_END), np.float32)
    cols[:, C_SIGN:C_SIGN + S] = np.sign((p % S)[:, None] - np.arange(S)[None, :])
    cols[:, C_IOTA:C_IOTA + S] = np.arange(S)[None, :]
    cols[:, C_U:C_U + TILES] = by_tile(a["condB_uprev"])
    cols[:, C_HEAD:C_HEAD + H4] = ((p % S) // DH)[:, None] == np.arange(H4)[None, :]
    cols[:, C_BQ:C_BQ + HG] = quads(a["L1_cond_bq"].reshape(HG, S).T)
    cols[:, C_BK:C_BK + HG] = quads(a["L1_cond_bk"].reshape(HG, S).T)
    cols[:, C_FC1B:C_FC1B + FC] = a["L3_cond_fc1_b"].reshape(FC, P).T
    cols[:, C_E2] = p // (P // E2)
    cols[:, C_E3] = np.minimum(p, E3 - 1)
    cols[:, C_BO] = a["L1_cond_bo"]
    by_head = lambda w: w.reshape(HG, H4, DH, -1).transpose(1, 0, 2, 3).reshape(D, -1)
    cols[:, C_BV] = by_head(a["L1_cond_bv"])[:, 0]
    cols[0:TH * A0, C_B1] = np.tile(a["L0_cond_b1"], TH)
    fb3 = np.zeros((E3 + 1, D), np.float32)
    fb3[0:E3, SHARED:] = a["L3_cond_experts_b"]
    fb3[E3, 0:SHARED] = a["L3_cond_fc2_b"]
    chunks = lambda w: w.T.reshape(FC, P, -1).transpose(1, 0, 2)

    arrays = {
        "xt": x.reshape(NBLK, TOK, D).transpose(0, 2, 1),
        "xn": x.reshape(NBLK, G, P, D).transpose(0, 2, 1, 3),
        "ints": ints, "bools": bools, "cols": cols,
        "w1": np.tile(a["L0_cond_W1"], (1, TH)), "vrep": np.tile(a["L0_cond_v"][:, None], (TH, P)),
        "wq": a["L1_cond_Wq"].T, "wk": a["L1_cond_Wk"].T, "wv": a["L1_cond_Wv"].T,
        "wo": by_head(a["L1_cond_Wo"].T),
        "wit": a["L2_cond_wi"].T, "wot": chunks(a["L2_cond_wo"]),
        "cwia": a["L2_cond_common_wi_a"], "cwibt": a["L2_cond_common_wi_b"].T,
        "cwoa": a["L2_cond_common_wo_a"], "cwobt": a["L2_cond_common_wo_b"].T,
        "ewiat": a["L2_cond_experts_wi_a"].reshape(P, D).T,
        "ewib": a["L2_cond_experts_wi_b"].transpose(0, 2, 1).reshape(P, F),
        "ewoat": chunks(a["L2_cond_experts_wo_a"].reshape(P, F)),
        "ewob": a["L2_cond_experts_wo_b"].transpose(0, 2, 1).reshape(P, D),
        "fc1t": a["L3_cond_fc1_w"].T, "fc2t": chunks(a["L3_cond_fc2_w"]),
        "e3t": a["L3_cond_experts_w"].reshape(E3, PART, FC, P).transpose(3, 0, 2, 1),
        "fb3": fb3, "ident_in": np.eye(P, dtype=np.float32),
    }
    nc = bacc.Bacc("TRN2", target_bir_lowering=False, num_devices=1)
    args = {}
    for name in arrays:
        arrays[name] = ca(arrays[name])
        args[name] = nc.dram_tensor(name + "_dram", arrays[name].shape, mybir.dt.from_np(arrays[name].dtype),
                                    kind="ExternalInput").ap()
    out = nc.dram_tensor("out_dram", (NBLK, P, G, D), F32, kind="ExternalOutput").ap()
    cond_resid_kernel(nc, out=out, **args)
    r = run_bass_kernel_spmd(nc, [{k + "_dram": v for k, v in arrays.items()}], core_ids=[0])
    got = r.results[0]["out_dram"]
    return np.ascontiguousarray(got.transpose(0, 2, 1, 3)).reshape(B, S, D)
```

```python
from contextlib import ExitStack

import concourse.bass as bass
from concourse import mybir

F32 = mybir.dt.float32
F32R = mybir.dt.float32r
I32 = mybir.dt.int32
U8 = mybir.dt.uint8
ALU = mybir.AluOpType
ACT = mybir.ActivationFunctionType
AX = mybir.AxisListType

P = 128
B = 128
S = 32
D = 128
Q4 = P // S
G = 4
TOK = G * P
NBLK = B * S // TOK
ROWS = G * Q4
TILES = B // Q4
A0 = 32
TH = 3
H = 16
DH = D // H
HG = 4
H4 = H // HG
F = 512
FC = F // P
RANK = 16
E2 = 8
E3 = 16
PART = 32
SHARED = D - PART
SCALE = DH ** -0.5
NEG = -1e30
LAM_MAX, LAM_RATE, ALPHA = 10.0, 5.0, 2.0

I_TYPE, I_E2, I_E3, I_IDX, I_END = 0, 32, 160, 288, 320
C_SIGN, C_IOTA, C_U, C_HEAD, C_BQ, C_BK, C_FC1B, C_E2, C_E3, C_BO, C_BV, C_B1, C_V, C_IDENT, C_END = (
    0, 32, 64, 96, 100, 104, 108, 112, 113, 114, 115, 116, 117, 117 + P, 117 + 2 * P)
A_W1, A_Q, A_K, A_V, A_O, A_END = 0, 96, 96 + D, 96 + 2 * D, 96 + 3 * D, 96 + 4 * D
R_IA, R_IB, R_OA, R_OB, R_FB, R_END = 0, D, D + F, D + 2 * F, 2 * D + 2 * F, 3 * D + 2 * F
W_EIA, W_EIB, W_EOB, W_FC1, W_EOA, W_I, W_O, W_END = (
    0, P, P + F, 2 * P + F, 2 * P + 2 * F, 2 * P + 3 * F, 2 * P + 4 * F, 2 * P + 5 * F)


def cond_resid_kernel(nc, xt, xn, ints, bools, cols, attn_w, rank_w, ffn_w, fc2t, e3t, out):
    with ExitStack() as ctx:
        def sb(name, shape, dt=F32):
            return ctx.enter_context(nc.sbuf_tensor(name, shape, dt))

        def bank(name):
            return ctx.enter_context(nc.psum_tensor(name, [P, 512], F32))

        def sem(name):
            return ctx.enter_context(nc.semaphore(name))

        ints_s = sb("ints_s", [P, I_END], I32)
        bools_s = sb("bools_s", [P, 2 * S // 4], I32)
        cols_s = sb("cols_s", [P, C_END])
        attn_s = sb("attn_s", [D, A_END])
        w1_s, wq_s, wk_s, wv_s, wo_s = (attn_s[:, a:b] for a, b in (
            (A_W1, A_Q), (A_Q, A_K), (A_K, A_V), (A_V, A_O), (A_O, A_END)))
        rank_s = sb("rank_s", [E3 + 1, R_END])
        ffn_s = sb("ffn_s", [P, W_END])
        vrep_s = cols_s[0:TH * A0, C_V:C_V + P]
        ident = cols_s[:, C_IDENT:C_IDENT + P]
        vpart = sb("vpart", [TH * A0, P], F32R)
        e3t_s = sb("e3t_s", [P, E3, FC, PART])

        def parts(name, shape):
            return sb(name + "_h", shape, F32R), sb(name + "_l", shape, F32R)

        ffn_p = parts("ffn", [P, W_END])

        intf = sb("intf", [P, I_END])
        neg_c = sb("neg_c", [P, TILES])
        masked = sb("masked", [P, TILES, S])
        cnt = sb("cnt", [P, TILES])
        idxm = sb("idxm", [P, S])
        mk = sb("mk", [P, 2 * S])
        ctab = sb("ctab", [P, S])
        ltab = sb("ltab", [P, S])
        ztab = sb("ztab", [P, S])
        ntab = sb("ntab", [P, S])
        lam = sb("lam", [P, TILES])
        sparse = sb("sparse", [P, TILES])
        dense = sb("dense", [P, TILES])
        bias = sb("bias", [P, TILES, S])
        hits = bias
        oh2 = sb("oh2", [P, B])
        oh3 = sb("oh3", [E3 + 1, B])
        e3i = sb("e3i", [P, B], I32)
        fbias = sb("fbias", [D, B])
        bo_eff = sb("bo_eff", [D, 1])
        spare = sb("spare", [P, 1])

        xT, xN = sb("xT", [D, TOK]), sb("xN", [P, G, D])
        th = sb("th", [TH * A0, TOK])
        thp = sb("thp", [TH * A0, TOK], F32R)
        l0s = sb("l0s", [P, G, S])
        l0e = sb("l0e", [P, G, S])
        l0m, l0d, l0r = sb("l0m", [P, G]), sb("l0d", [P, G]), sb("l0r", [P, G])
        l0c = sb("l0c", [P, G])
        poolP = sb("poolP", [P, G, P])
        x1T = sb("x1T", [D, TOK])
        qf = sb("qf", [P, TOK])
        qb = sb("qb", [P, HG, G, P])
        kb = sb("kb", [P, HG, H4, G, S])
        vb = sb("vb", [P, G, H, Q4, DH + 1])
        sc = sb("sc", [P, 2, H, S])
        rmax = sb("rmax", [P, 2, H])
        ex = sb("ex", [P, 2, H, S])
        pt = sb("pt", [P, 2, H, S])
        rc = sb("rc", [P, 2, HG, Q4])
        on = sb("on", [P, 2, Q4, HG, DH])
        oT = sb("oT", [P, G, P])
        x2T = sb("x2T", [D, TOK])
        x2p = parts("x2", [D, TOK])

        lowm, lowm2 = sb("lowm", [P, TOK]), sb("lowm2", [P, TOK])
        lowp, lowp2 = parts("lowp", [P, TOK]), parts("lowp2", [P, TOK])
        hid = parts("hid", [P, FC, TOK])
        x3T = sb("x3T", [D, TOK])
        x3p = parts("x3", [D, TOK])
        x3b = sb("x3b", [D, TOK])
        x3n = sb("x3n", [P, TOK])
        hT = sb("hT", [P, FC, TOK])
        btmp = hT[:, 0:2, :].rearrange("p c (r s) -> p (c r) s", s=S)
        rw = sb("rw", [P, ROWS, FC, D])
        o_s = sb("o_s", [P, G, D])

        pA0, pA1, pS0, pS1, pV, pB0, pB1, pB2 = (
            bank(n) for n in ("pA0", "pA1", "pS0", "pS1", "pV", "pB0", "pB1", "pB2"))
        pS = [pS0, pS1]
        HID = [pB1, pB2, pB0, pB1]
        GIN = [pB1, pB2, pS0, pS1]

        ld_small, ld_attn, ld_ffn, ld_rw = sem("ld_small"), sem("ld_attn"), sem("ld_ffn"), sem("ld_rw")
        ld_xT, ld_xN, st_out = sem("ld_xT"), sem("ld_xN"), sem("st_out")
        prep = sem("prep")
        w_high, w_low = sem("w_high"), sem("w_low")
        bias_sb = sem("bias_sb")
        prep_act, prep_pe, prep_pool = sem("prep_act"), sem("prep_pe"), sem("prep_pool")
        tables = sem("tables")
        h_ps, th_sb, thl_sb, s_ps = sem("h_ps"), sem("th_sb"), sem("thl_sb"), sem("s_ps")
        l0_step, l0_exp, pool_ps, x1_sb = sem("l0_step"), sem("l0_exp"), sem("pool_ps"), sem("x1_sb")
        q_ps, k_ps, v_ps = sem("q_ps"), sem("k_ps"), sem("v_ps")
        qf_sb, q_sb, k_sb, v_sb = sem("qf_sb"), sem("q_sb"), sem("k_sb"), sem("v_sb")
        sc_ps, sc_sb, mx_sb = sem("sc_ps"), sem("sc_sb"), sem("mx_sb")
        sub_sb, ex_sb, pt_sb, pv_ps = sem("sub_sb"), sem("ex_sb"), sem("pt_sb"), sem("pv_ps")
        rc_sb, on_sb, o_sb = sem("rc_sb"), sem("on_sb"), sem("o_sb")
        wo_ps, x2_sb, x2h_sb, x2l_sb = sem("wo_ps"), sem("x2_sb"), sem("x2h_sb"), sem("x2l_sb")
        low_ps, low_sb, lowl_sb = sem("low_ps"), sem("low_sb"), sem("lowl_sb")
        low2_ps, low2_sb, lowl2_sb = sem("low2_ps"), sem("low2_sb"), sem("lowl2_sb")
        hid_ps, hid_sb, hidl_sb = sem("hid_ps"), sem("hid_sb"), sem("hidl_sb")
        out_ps, x3_sb, x3b_sb = sem("out_ps"), sem("x3_sb"), sem("x3b_sb")
        x3l_sb, x3t_ps, x3n_sb = sem("x3l_sb"), sem("x3t_ps"), sem("x3n_sb")
        g_ps, g_sb = sem("g_ps"), sem("g_sb")
        rw_sb, fin_ps, res_sb = sem("rw_sb"), sem("fin_ps"), sem("res_sb")

        def at(eng, s, value):
            if isinstance(value, int) and value <= 0:
                return
            eng.wait_ge(s, value)

        N_SMALL, N_ATTN, N_FFN, N_RW = 3, 2, 2, 1 + FC
        PREP_VEC = [0]

        def bias_steps(first, last):
            n = last - first

            def by_token(x):
                return x[:, :].unsqueeze(1).to_broadcast([P, n, S])

            def by_tile(x):
                return x[:, first:last].unsqueeze(2).to_broadcast([P, n, S])

            b, t = bias[:, first:last, :], btmp[:, first:last, :]
            return ((b, by_token(ltab), by_tile(sparse), ALU.mult),
                    (t, by_token(ntab), by_tile(dense), ALU.mult), (b, b, t, ALU.add))

        block = ctx.enter_context(nc.Block())

        @block.sync
        def _(sp):
            sp.dma_start(ints_s[:, :], ints).then_inc(ld_small, 16)
            sp.dma_start(bools_s[:, :], bools).then_inc(ld_small, 16)
            sp.dma_start(cols_s[:, :], cols).then_inc(ld_small, 16)

            def load_xT(i):
                at(sp, x1_sb, i)
                sp.dma_start(xT[:, :], xt[i]).then_inc(ld_xT, 16)

            def load_xN(i):
                at(sp, pool_ps, i)
                sp.dma_start(xN[:, :, :], xn[i]).then_inc(ld_xN, 16)

            def load_x(i):
                load_xT(i)
                load_xN(i)

            def store(i):
                at(sp, res_sb, i + 1)
                sp.dma_start(out[i], o_s[:, :, :]).then_inc(st_out, 16)

            sp.sem_inc(st_out, 16)
            load_xT(0)
            for dst, src in ((attn_s, attn_w), (rank_s, rank_w)):
                sp.dma_start(dst[:, :], src).then_inc(ld_attn, 16)
            load_xN(0)
            for a, b in ((0, W_I), (W_I, W_END)):
                sp.dma_start(ffn_s[:, a:b], ffn_w[:, a:b]).then_inc(ld_ffn, 16)
            load_x(1)
            sp.dma_start(e3t_s[:, :, :, :], e3t).then_inc(ld_rw, 16)
            for c in range(FC):
                sp.dma_start(rw[:, :, c, 0:SHARED],
                             fc2t[:, c, :].unsqueeze(1).to_broadcast([P, ROWS, SHARED])).then_inc(ld_rw, 16)
            load_x(2)
            with sp.Fori(3, NBLK) as n:
                load_x(n)
                store(n - 3)
            store(NBLK - 3)
            store(NBLK - 2)
            store(NBLK - 1)
            sp.wait_ge(st_out, 16 * (NBLK + 1))

        @block.gpsimd
        def _(pool):
            pool.memset(poolP[:, :, :], 0.0).then_inc(prep_pool, 1)
            pool.memset(qb[:, :, :, :], 0.0).then_inc(prep_pool, 1)
            pool.memset(vb[:, :, :, :, :], 0.0).then_inc(prep_pool, 1)
            pool.wait_ge(prep_pool, 3)
            for q in range(Q4):
                pool.memset(vb[S * q:S * q + S, :, :, q, DH:DH + 1], 1.0).then_inc(prep_pool, 1)

            def subtract_max(i, g):
                at(pool, mx_sb, G * i + g + 1)
                pool.tensor_tensor(sc[:, g % 2, :, :], sc[:, g % 2, :, :],
                                   rmax[:, g % 2, :].unsqueeze(2).to_broadcast([P, H, S]),
                                   ALU.subtract).then_inc(sub_sb, 1)

            def queries(i):
                at(pool, qf_sb, i + 1)
                for q in range(Q4):
                    k = slice(S * q, S * q + S)
                    pool.tensor_tensor(
                        qb[k, :, :, k], qf[k, :].rearrange("p (a g s) -> p a g s", a=HG, g=G),
                        cols_s[k, C_BQ:C_BQ + HG].unsqueeze(2).unsqueeze(3).to_broadcast([S, HG, G, S]),
                        ALU.add).then_inc(q_sb, 1)
                at(pool, q_sb, Q4 * (i + 1))

            def biased_x3(i):
                at(pool, x3_sb, 2 * i + 1)
                at(pool, x3t_ps, i)
                pool.tensor_tensor(x3b[:, :].rearrange("p (r s) -> p r s", s=S),
                                   x3T[:, :].rearrange("p (r s) -> p r s", s=S),
                                   fbias[:, bass.ds(ROWS * i, ROWS)].unsqueeze(2).to_broadcast([P, ROWS, S]),
                                   ALU.add).then_inc(x3b_sb, 1)

            def expert_weights(i, part):
                if part == 0:
                    at(pool, fin_ps, i + 1)
                for r in range(Q4 * part, Q4 * part + Q4):
                    e = pool.value_load(e3i[0:1, bass.ds(ROWS * i + r, 1)], min_val=0, max_val=E3 - 1)
                    pool.tensor_copy(rw[:, r, :, SHARED:D],
                                     e3t_s[:, bass.ds(e, 1), :, :].rearrange("p o c n -> p (o c) n"))\
                        .then_inc(rw_sb, 1)

            def weight_lows(first, last, n):
                at(pool, w_high, n)
                pool.tensor_tensor(ffn_p[1][:, first:last], ffn_s[:, first:last], ffn_p[0][:, first:last],
                                   ALU.subtract).then_inc(w_low, 1)

            pool.wait_ge(prep_pool, 3 + Q4)
            weight_lows(0, W_I, 1)
            pool.wait_ge(w_low, 1)
            queries(0)
            subtract_max(0, 0)
            subtract_max(0, 1)
            subtract_max(0, 2)
            subtract_max(0, 3)
            weight_lows(W_I, W_END, 2)
            of_sparse, of_dense, both = bias_steps(G, TILES)
            pool.wait_ge(prep, P_BIAS)
            pool.tensor_tensor(*of_sparse).then_inc(bias_sb, 1)
            pool.tensor_tensor(*of_dense).then_inc(bias_sb, 1)
            pool.wait_ge(bias_sb, 2)
            pool.tensor_tensor(*both).then_inc(bias_sb, 1)

            def step_of(n):
                at(pool, x3b_sb, n - 1)
                if isinstance(n, int) and n == 1:
                    pool.wait_ge(bias_sb, 3)
                queries(n)
                if isinstance(n, int) and n == 1:
                    pool.wait_ge(ld_rw, 16 * N_RW)
                subtract_max(n, 0)
                subtract_max(n, 1)
                expert_weights(n - 1, 0)
                subtract_max(n, 2)
                expert_weights(n - 1, 1)
                subtract_max(n, 3)
                expert_weights(n - 1, 2)
                expert_weights(n - 1, 3)
                biased_x3(n - 1)

            step_of(1)
            with pool.Fori(2, NBLK) as n:
                step_of(n)
            for part in range(G):
                expert_weights(NBLK - 1, part)
            biased_x3(NBLK - 1)

        @block.scalar
        def _(act):
            act.wait_ge(ld_small, 16 * N_SMALL)
            act.activation(lam[:, :], cols_s[:, C_U:C_U + TILES], ACT.Exp, scale=-LAM_RATE).then_inc(prep_act, 1)

            def tanh(i):
                at(act, h_ps, i + 1)
                for dst in (thp, th):
                    act.activation(dst[:, :], pV[0:TH * A0, :], ACT.Tanh,
                                   bias=cols_s[0:TH * A0, C_B1:C_B1 + 1]).then_inc(th_sb, 1)

            def l0_exps(i):
                at(act, l0_step, L0_STEPS * i + 6)
                act.activation(l0e[:, :, :], l0s[:, :, :], ACT.Exp).then_inc(l0_exp, 1)

            def queries(i):
                at(act, q_ps, i + 1)
                at(act, q_sb, Q4 * i)
                act.activation(qf[:, :], pA1[:, :], ACT.Copy).then_inc(qf_sb, 1)

            def values(i):
                at(act, v_ps, i + 1)
                for q in range(Q4):
                    part = slice(S * q, S * q + S)
                    act.activation(vb[part, :, :, q, 0:DH].rearrange("p g h d -> p (g h) d"),
                                   pV[part, :].rearrange("p (n d) -> p n d", d=DH), ACT.Copy).then_inc(v_sb, 1)

            def exps(i, g):
                t = G * i + g
                at(act, sub_sb, t + 1)
                at(act, pt_sb, t - 1)
                act.activation(ex[:, g % 2, :, :], sc[:, g % 2, :, :], ACT.Exp).then_inc(ex_sb, 1)

            def relu(i, c):
                at(act, hid_ps, FC * i + c + 1)
                act.activation(hid[0][:, c, :], HID[c][:, :], ACT.Relu).then_inc(hid_sb, 1)

            def gelu(i, c):
                at(act, g_ps, FC * i + c + 1)
                act.activation(hT[:, c, :], GIN[c][:, :], ACT.Gelu,
                               bias=cols_s[:, C_FC1B + c:C_FC1B + c + 1]).then_inc(g_sb, 1)

            def x2_high(i):
                at(act, x2_sb, i + 1)
                act.activation(x2p[0][:, :], x2T[:, :], ACT.Copy).then_inc(x2h_sb, 1)

            def table(n, function):
                at(act, tables, 2 * n - (2 if function is ACT.Exp else 1))
                act.activation(spare[:, :], cols_s[:, C_IOTA:C_IOTA + 1], function).then_inc(tables, 1)

            def token_major(i):
                at(act, x3t_ps, i + 1)
                act.activation(x3n[:, :], pB0[:, :], ACT.Copy).then_inc(x3n_sb, 1)

            act.wait_ge(prep_pool, 3 + Q4)
            tanh(0)
            l0_exps(0)
            act.wait_ge(ld_ffn, 16 * N_FFN)
            act.activation(ffn_p[0][:, 0:W_I], ffn_s[:, 0:W_I], ACT.Copy).then_inc(w_high, 1)
            act.wait_ge(prep, P_COUNT)
            act.activation(ltab[:, :], ctab[:, :], ACT.Ln).then_inc(prep_act, 1)
            queries(0)
            act.wait_ge(prep, P_PRODUCTS)
            act.activation(ffn_p[0][:, W_I:W_END], ffn_s[:, W_I:W_END], ACT.Copy).then_inc(w_high, 1)
            tanh(1)
            values(0)
            for g in range(G):
                exps(0, g)
            l0_exps(1)
            x2_high(0)

            def step_of(n, last, next_block=True):
                queries(n)
                table(n, ACT.Exp)
                if next_block:
                    tanh(n + 1)
                if last is not None:
                    token_major(last)
                if next_block:
                    l0_exps(n + 1)
                exps(n, 0)
                values(n)
                exps(n, 1)
                relu(n - 1, 0)
                relu(n - 1, 1)
                exps(n, 2)
                relu(n - 1, 2)
                relu(n - 1, 3)
                exps(n, 3)
                table(n, ACT.Gelu)
                x2_high(n)
                for c in range(FC):
                    gelu(n - 1, c)

            step_of(1, None)
            with act.Fori(2, NBLK - 1) as n:
                step_of(n, n - 2)
            step_of(NBLK - 1, NBLK - 3, False)
            token_major(NBLK - 2)
            for c in range(FC):
                relu(NBLK - 1, c)
            for c in range(FC):
                gelu(NBLK - 1, c)
            token_major(NBLK - 1)

        @block.tensor
        def _(pe):
            mm = pe.matmul

            def scorer_in(i):
                at(pe, ld_xT, 16 * (i + 1))
                at(pe, x2_sb, i - 1)
                mm(pV[0:TH * A0, :], w1_s[:, :], xT[:, :], start=True, stop=True).then_inc(h_ps, 1)

            def scorer_out(i):
                at(pe, thl_sb, i + 1)
                at(pe, qf_sb, i)
                mm(pA1[:, :], vpart[:, :], thp[:, :], start=True, stop=True).then_inc(s_ps, 1)

            def pooling(i):
                at(pe, ld_xN, 16 * (i + 1))
                at(pe, l0_step, L0_STEPS * (i + 1))
                at(pe, k_sb, HG * i)
                for g in range(G):
                    last = mm(pA0[:, P * g:P * g + P], xN[:, g, :], poolP[:, g, :], start=True, stop=True)
                last.then_inc(pool_ps, 1)

            def project(i, ps, w, done):
                at(pe, x1_sb, i + 1)
                rows = x1T[:, :].rearrange("p (g q s) -> p g q s", g=G, q=Q4)
                for hg in range(HG):
                    for q in range(Q4):
                        last = mm(ps[S * q:S * q + S, P * hg:P * hg + P], w[:, S * hg:S * hg + S],
                                  rows[:, :, q, :], start=True, stop=True)
                last.then_inc(done, 1)

            def queries(i):
                project(i, pA1, wq_s, q_ps)

            def keys(i):
                project(i, pA0, wk_s, k_ps)

            def values(i):
                at(pe, th_sb, 2 * min(i + 2, NBLK) if isinstance(i, int) else 2 * (i + 2))
                for g in range(G):
                    last = mm(pV[:, P * g:P * g + P], x1T[:, P * g:P * g + P], wv_s[:, :], start=True, stop=True)
                last.then_inc(v_ps, 1)

            def scores(i, g):
                if g == 0:
                    at(pe, q_sb, Q4 * (i + 1))
                    at(pe, k_sb, HG * (i + 1))
                    at(pe, g_sb, FC * (i - 1))
                at(pe, sc_sb, G * i + g - 1)
                for hg in range(HG):
                    last = mm(pS[g % 2][:, P * hg:P * hg + P], qb[:, hg, g, :], kb[:, hg, :, g, :],
                              start=True, stop=True)
                last.then_inc(sc_ps, 1)

            def weigh(i, g):
                at(pe, pt_sb, G * i + g + 1)
                if g == 0:
                    at(pe, v_sb, Q4 * (i + 1))
                if g == 2:
                    at(pe, on_sb, G * i + 2)
                w = Q4 * (DH + 1)
                for hg in range(HG):
                    for h4 in range(H4):
                        h = H4 * hg + h4
                        at_col = (g % 2) * HG * w + hg * w
                        last = mm(pV[S * h4:S * h4 + S, at_col:at_col + w], pt[:, g % 2, h, :],
                                  vb[:, g, h, :, :], start=True, stop=True)
                last.then_inc(pv_ps, 1)

            def attn_out(i):
                at(pe, o_sb, G // 2 * (i + 1))
                mm(pV[:, :], wo_s[:, :], oT[:, :, :], start=True, stop=True).then_inc(wo_ps, 1)

            def parts3(ps, w, x, start, stop, low=None):
                mm(ps, w[0], x[0], start=start, stop=False)
                mm(ps, w[1], x[0], start=False, stop=False)
                if low is not None:
                    at(pe, *low)
                return mm(ps, w[0], x[1], start=False, stop=stop)

            def weight(first, c=0):
                return [w[:, first + P * c:first + P * c + P] for w in ffn_p]

            def chunk(pair, c):
                return [w[:, c, :] for w in pair]

            def whole(pair):
                return [w[:, :] for w in pair]

            def low(i):
                at(pe, x2h_sb, i + 1)
                at(pe, x3_sb, 2 * i - 1)
                parts3(pB0[:, :], weight(W_EIA), whole(x2p), True, True, (x2l_sb, i + 1)).then_inc(low_ps, 1)

            def hidden(i, c):
                if c == 1:
                    at(pe, res_sb, i)
                if c == 2:
                    at(pe, x3n_sb, i)
                if c == 3:
                    at(pe, hidl_sb, FC * i + 1)
                parts3(HID[c][:, :], weight(W_I, c), whole(x2p), True, False)

            def hidden_expert(i, c):
                at(pe, low_sb, 2 * (i + 1))
                parts3(HID[c][:, :], weight(W_EIB, c), whole(lowp), False, True, (lowl_sb, i + 1)).then_inc(hid_ps, 1)

            def low2(i):
                at(pe, hidl_sb, FC * i + 2)
                for c in range(FC):
                    at(pe, hid_sb, FC * i + c + 1)
                    last = parts3(pB2[:, :], weight(W_EOA, c), chunk(hid, c), c == 0, c == FC - 1,
                                  (hidl_sb, FC * i + c + 1))
                last.then_inc(low2_ps, 1)

            def out2(i):
                for c in range(FC):
                    parts3(pB0[:, :], weight(W_O, c), chunk(hid, c), c == 0, False)

            def out2_expert(i):
                at(pe, low2_sb, 2 * (i + 1))
                parts3(pB0[:, :], weight(W_EOB), whole(lowp2), False, True, (lowl2_sb, i + 1)).then_inc(out_ps, 1)

            def fc1(i, c):
                if c == 0:
                    at(pe, x3_sb, 2 * (i + 1))
                if c == 2:
                    at(pe, sc_sb, G * NBLK if isinstance(i, int) and i == NBLK - 1 else G * (i + 2))
                parts3(GIN[c][:, :], weight(W_FC1, c), whole(x3p), True, True, (x3l_sb, i + 1)).then_inc(g_ps, 1)

            def token_major(i):
                at(pe, x3b_sb, i + 1)
                at(pe, low_sb, 2 * NBLK if isinstance(i, int) and i == NBLK - 1 else 2 * (i + 2) - 1)
                for g in range(G):
                    last = pe.transpose(pB0[:, P * g:P * g + P], x3b[:, P * g:P * g + P], ident[:, :])
                last.then_inc(x3t_ps, 1)

            def final(i, g):
                if g == 0:
                    at(pe, rw_sb, ROWS * (i + 1))
                    at(pe, g_sb, FC * (i + 1))
                for c in range(FC):
                    for q in range(Q4):
                        tok = slice(P * g + S * q, P * g + S * q + S)
                        last = mm(pB2[S * q:S * q + S, P * g:P * g + P], hT[:, c, tok],
                                  rw[:, Q4 * g + q, c, :], start=(c == 0), stop=(c == FC - 1))
                if g == G - 1:
                    last.then_inc(fin_ps, 1)

            def factor(first, width):
                return rank_s[0:RANK, first:first + width]

            def prepare_wi():
                mm(pB0[:, :], factor(R_IA, D), factor(R_IB, F), start=True, stop=True).then_inc(prep_pe, 1)

            def prepare_wo():
                for c in range(FC):
                    last = mm(pB1[:, P * c:P * c + P], factor(R_OA + P * c, P), factor(R_OB, D), start=True, stop=True)
                last.then_inc(prep_pe, 1)
                mm(pB2[:, 0:1], wo_s[:, :], cols_s[:, C_BV:C_BV + 1], start=True, stop=True).then_inc(prep_pe, 1)

            def prepare_last_bias():
                pe.wait_ge(prep, P_E3)
                mm(pB2[:, P:P + B], rank_s[:, R_FB:R_END], oh3[:, :], start=True, stop=True).then_inc(prep_pe, 1)

            pe.wait_ge(ld_small, 16 * N_SMALL)
            pe.wait_ge(ld_attn, 16 * N_ATTN)
            pe.sem_inc(fin_ps, 1)
            scorer_in(0)
            prepare_wi()
            scorer_out(0)
            prepare_wo()
            pe.wait_ge(prep_pool, 3 + Q4)
            pooling(0)
            prepare_last_bias()
            queries(0)
            keys(0)
            scorer_in(1)
            values(0)
            scores(0, 0)
            scores(0, 1)
            scorer_out(1)
            scores(0, 2)
            scores(0, 3)
            weigh(0, 0)
            weigh(0, 1)
            weigh(0, 2)
            weigh(0, 3)
            attn_out(0)
            pooling(1)

            def step_of(n, last, next_block=True):
                if last is None:
                    pe.wait_ge(w_low, 2)
                low(n - 1)
                queries(n)
                keys(n)
                if last is not None:
                    token_major(last)
                if next_block:
                    scorer_in(n + 1)
                if last is not None:
                    final(last, 0)
                    final(last, 1)
                else:
                    hidden(n - 1, 0)
                    hidden_expert(n - 1, 0)
                if next_block:
                    scorer_out(n + 1)
                if last is not None:
                    final(last, 2)
                scores(n, 0)
                scores(n, 1)
                if last is not None:
                    final(last, 3)
                values(n)
                if last is not None:
                    hidden(n - 1, 0)
                    hidden_expert(n - 1, 0)
                scores(n, 2)
                hidden(n - 1, 1)
                hidden_expert(n - 1, 1)
                scores(n, 3)
                weigh(n, 0)
                hidden(n - 1, 2)
                hidden_expert(n - 1, 2)
                weigh(n, 1)
                hidden(n - 1, 3)
                hidden_expert(n - 1, 3)
                weigh(n, 2)
                low2(n - 1)
                weigh(n, 3)
                out2(n - 1)
                out2_expert(n - 1)
                if next_block:
                    pooling(n + 1)
                attn_out(n)
                for c in range(FC):
                    fc1(n - 1, c)

            step_of(1, None)
            with pe.Fori(2, NBLK - 1) as n:
                step_of(n, n - 2)
            step_of(NBLK - 1, NBLK - 3, False)
            low(NBLK - 1)
            token_major(NBLK - 2)
            for g in range(G):
                final(NBLK - 2, g)
            for c in range(FC):
                hidden(NBLK - 1, c)
                hidden_expert(NBLK - 1, c)
            low2(NBLK - 1)
            out2(NBLK - 1)
            out2_expert(NBLK - 1)
            for c in range(FC):
                fc1(NBLK - 1, c)
            token_major(NBLK - 1)
            for g in range(G):
                final(NBLK - 1, g)

        @block.vector
        def _(dve):
            tt, ts, stt = dve.tensor_tensor, dve.tensor_scalar, dve.scalar_tensor_tensor

            def step(ins):
                PREP_VEC[0] += 1
                ins.then_inc(prep, 1)
                dve.wait_ge(prep, PREP_VEC[0])

            def wrap(col, width, n):
                x, t = intf[:, col:col + width], btmp[:, 0:4, :].rearrange("p a b -> p (a b)")[:, 0:width]
                step(ts(t, x, 0.0, float(n), ALU.is_lt, ALU.mult))
                step(tt(x, x, t, ALU.add))
                step(ts(x, x, 0.0, float(n - 1), ALU.max, ALU.min))

            def prepare_pooling():
                dve.wait_ge(ld_small, 16 * N_SMALL)
                step(dve.tensor_copy(intf[:, :], ints_s[:, :]))
                step(ts(cnt[:, :], intf[:, I_TYPE:I_TYPE + TILES], 0.0, None, ALU.is_equal))
                step(stt(neg_c[:, :], intf[:, I_TYPE:I_TYPE + TILES], 1.0, cnt[:, :], ALU.is_equal, ALU.subtract))
                mask_tokens(0, G)
                count_tokens(0, G)
                two = 2 * A0
                step(dve.tensor_copy(vpart[:, :], vrep_s[:, :]))
                step(tt(vpart[two:, :], vrep_s[two:, :], vpart[two:, :], ALU.subtract))

            def mask_tokens(first, last):
                n = last - first
                step(tt(masked[:, first:last, :], cols_s[:, C_SIGN:C_SIGN + S].unsqueeze(1).to_broadcast([P, n, S]),
                        neg_c[:, first:last].unsqueeze(2).to_broadcast([P, n, S]), ALU.is_equal))

            def count_tokens(first, last):
                c = cnt[:, first:last]
                step(dve.tensor_reduce(c, masked[:, first:last, :], AX.X, ALU.add))
                step(ts(c, c, -1.0, float(S), ALU.mult, ALU.add))

            def prepare_ids():
                step(dve.tensor_copy(e3i[:, :], intf[:, I_E3:I_E3 + B]))
                step(ts(oh3[:, :], intf[0:E3 + 1, I_E3:I_E3 + B], cols_s[0:E3 + 1, C_E3:C_E3 + 1], None, ALU.is_equal))
                assert PREP_VEC[0] == P_E3
                step(ts(oh2[:, :], intf[:, I_E2:I_E2 + B], cols_s[:, C_E2:C_E2 + 1], ALPHA, ALU.is_equal, ALU.mult))

            def prepare_hits():
                step(dve.tensor_copy(mk[:, :], bools_s[:, :].bitcast(U8)))
                wrap(I_IDX, S, S)
                step(stt(idxm[:, :], intf[:, I_IDX:I_IDX + S], 1.0, mk[:, S:2 * S], ALU.add, ALU.mult))
                step(ts(idxm[:, :], idxm[:, :], -1.0, None, ALU.add))
                step(tt(hits[:, :, :], idxm[:, :].unsqueeze(1).to_broadcast([P, S, S]),
                        cols_s[:, C_IOTA:C_IOTA + S].unsqueeze(2).to_broadcast([P, S, S]), ALU.is_equal))

            def prepare_counts():
                step(dve.tensor_reduce(ntab[:, :], hits[:, :, :], AX.X, ALU.add))
                step(ts(ctab[:, :], ntab[:, :], 1.0, None, ALU.max))
                assert PREP_VEC[0] == P_COUNT

            def prepare_strength():
                step(ts(ztab[:, :], ntab[:, :], -0.5, -2 * NEG, ALU.add, ALU.mult))
                step(ts(ntab[:, :], mk[:, 0:S], -1.0, None, ALU.add))
                dve.wait_ge(prep_act, 1)
                step(ts(lam[:, :], lam[:, :], LAM_MAX, 2.0, ALU.mult, ALU.min))
                step(ts(sparse[:, :], lam[:, :], 1.0, None, ALU.is_ge))
                step(stt(dense[:, :], lam[:, :], 1.0, lam[:, :], ALU.is_lt, ALU.mult))

            def prepare_bias():
                dve.wait_ge(prep_act, 2)
                step(tt(ltab[:, :], ltab[:, :], ztab[:, :], ALU.min))
                for args in bias_steps(0, G):
                    step(tt(*args))
                assert PREP_VEC[0] == P_BIAS

            def prepare_products():
                dve.wait_ge(prep_pe, 4)
                dve.wait_ge(ld_ffn, 16 * N_FFN)
                for first, ps in ((W_I, pB0), (W_O, pB1)):
                    w = ffn_s[:, first:first + F]
                    step(stt(w, ps[:, :], ALPHA, w, ALU.mult, ALU.add))
                assert PREP_VEC[0] == P_PRODUCTS
                step(tt(bo_eff[:, :], pB2[:, 0:1], cols_s[:, C_BO:C_BO + 1], ALU.add))
                step(dve.tensor_copy(fbias[:, :], pB2[:, P:P + B]))

            def scorer_low(i):
                at(dve, th_sb, 2 * (i + 1))
                tt(thp[A0:2 * A0, :], th[A0:2 * A0, :], thp[A0:2 * A0, :], ALU.subtract).then_inc(thl_sb, 1)

            def pool_weights(i, part):
                n = L0_STEPS * i
                if part == 0:
                    at(dve, s_ps, i + 1)
                    tok = pA1[:, :].rearrange("p (g q l) -> p g q l", g=G, q=Q4)
                    for q in range(Q4):
                        k = slice(S * q, S * q + S)
                        stt(l0s[k, :, :], masked[k, bass.ds(G * i, G), :], NEG, tok[k, :, q, :],
                            ALU.mult, ALU.add).then_inc(l0_step, 1)
                    at(dve, l0_step, n + 4)
                    dve.tensor_reduce(l0m[:, :], l0s[:, :, :], AX.X, ALU.max).then_inc(l0_step, 1)
                    at(dve, l0_step, n + 5)
                    tt(l0s[:, :, :], l0s[:, :, :], l0m[:, :].unsqueeze(2).to_broadcast([P, G, S]),
                       ALU.subtract).then_inc(l0_step, 1)
                    return
                at(dve, l0_exp, i + 1)
                dve.tensor_reduce(l0d[:, :], l0e[:, :, :], AX.X, ALU.add).then_inc(l0_step, 1)
                at(dve, l0_step, n + 7)
                tt(l0r[:, :], l0d[:, :], cnt[:, bass.ds(G * i, G)], ALU.mult).then_inc(l0_step, 1)
                at(dve, l0_step, n + 8)
                dve.reciprocal(l0c[:, :], l0r[:, :]).then_inc(l0_step, 1)
                at(dve, l0_step, n + 9)
                tt(l0e[:, :, :], l0e[:, :, :], l0c[:, :].unsqueeze(2).to_broadcast([P, G, S]),
                   ALU.mult).then_inc(l0_step, 1)
                at(dve, l0_step, n + 10)
                for q in range(Q4):
                    k = slice(S * q, S * q + S)
                    dve.transpose(poolP[k, :, k], l0e[k, :, :]).then_inc(l0_step, 1)

            def x1(i):
                at(dve, pool_ps, i + 1)
                at(dve, x2_sb, i)
                tt(x1T[:, :], pA0[:, :], xT[:, :], ALU.add).then_inc(x1_sb, 1)

            def keys(i):
                at(dve, k_ps, i + 1)
                for hg in range(HG):
                    stt(kb[:, hg, :, :, :].rearrange("p h g t -> p h (g t)"),
                        pA0[:, P * hg:P * hg + P].unsqueeze(1).to_broadcast([P, H4, P]),
                        cols_s[:, C_BK + hg:C_BK + hg + 1],
                        cols_s[:, C_HEAD:C_HEAD + H4].unsqueeze(2).to_broadcast([P, H4, P]),
                        ALU.add, ALU.mult).then_inc(k_sb, 1)

            def score_max(i, g):
                t = G * i + g
                at(dve, sc_ps, t + 1)
                at(dve, ex_sb, t - 1)
                stt(sc[:, g % 2, :, :], pS[g % 2][:, :].rearrange("p (h t) -> p h t", t=S), SCALE,
                    bias[:, bass.ds(t, 1), :].to_broadcast([P, H, S]), ALU.mult, ALU.add).then_inc(sc_sb, 1)
                at(dve, sc_sb, t + 1)
                dve.tensor_reduce(rmax[:, g % 2, :], sc[:, g % 2, :, :], AX.X, ALU.max).then_inc(mx_sb, 1)

            def turn(i, g):
                t = G * i + g
                at(dve, ex_sb, t + 1)
                at(dve, pv_ps, t - 1)
                dve.transpose(pt[:, g % 2, :, :], ex[:, g % 2, :, :]).then_inc(pt_sb, 1)

            def normalise(i, pair):
                n = G // 2 * i + pair
                at(dve, pv_ps, 2 * n + 2)
                sums = pV[:, 0:2 * H * (DH + 1)].rearrange("p (n d) -> p n d", d=DH + 1)
                dve.reciprocal(rc[:, :, :, :].rearrange("p t a q -> p (t a q)"), sums[:, :, DH]).then_inc(rc_sb, 1)
                at(dve, rc_sb, n + 1)
                for t in range(2):
                    tt(on[:, t, :, :, :].rearrange("p q a d -> p a q d"),
                       sums[:, H * t:H * t + H, 0:DH].rearrange("p (a q) d -> p a q d", q=Q4),
                       rc[:, t, :, :].unsqueeze(3).to_broadcast([P, HG, Q4, DH]), ALU.mult).then_inc(on_sb, 1)
                at(dve, on_sb, 2 * n + 2)
                dve.transpose(oT[:, 2 * pair:2 * pair + 2, :],
                              on[:, :, :, :, :].rearrange("p t q a d -> p t (q a d)")).then_inc(o_sb, 1)

            def x2(i):
                at(dve, wo_ps, i + 1)
                stt(x2T[:, :], pV[:, :], bo_eff[:, 0:1], x1T[:, :], ALU.add, ALU.add).then_inc(x2_sb, 1)

            def x2_low(i):
                at(dve, x2h_sb, i + 1)
                tt(x2p[1][:, :], x2T[:, :], x2p[0][:, :], ALU.subtract).then_inc(x2l_sb, 1)

            def rows_of(x, i):
                return x[:, bass.ds(ROWS * i, ROWS)].unsqueeze(2).to_broadcast([P, ROWS, S])

            def by_row(x):
                return x[:, :].rearrange("p (r s) -> p r s", s=S)

            def mask_low(i):
                at(dve, low_ps, i + 1)
                tt(by_row(lowm), by_row(pB0), rows_of(oh2, i), ALU.mult).then_inc(low_sb, 1)
                at(dve, low_sb, 2 * i + 1)
                dve.tensor_copy(lowp[0][:, :], lowm[:, :]).then_inc(low_sb, 1)
                at(dve, low_sb, 2 * i + 2)
                tt(lowp[1][:, :], lowm[:, :], lowp[0][:, :], ALU.subtract).then_inc(lowl_sb, 1)

            def mask_low2(i):
                at(dve, low2_ps, i + 1)
                tt(by_row(lowm2), by_row(pB2), rows_of(oh2, i), ALU.mult).then_inc(low2_sb, 1)
                at(dve, low2_sb, 2 * i + 1)
                dve.tensor_copy(lowp2[0][:, :], lowm2[:, :]).then_inc(low2_sb, 1)
                at(dve, low2_sb, 2 * i + 2)
                tt(lowp2[1][:, :], lowm2[:, :], lowp2[0][:, :], ALU.subtract).then_inc(lowl2_sb, 1)

            def relu_low(i, c):
                at(dve, hid_sb, FC * i + c + 1)
                stt(hid[1][:, c, :], HID[c][:, :], 0.0, hid[0][:, c, :],
                    ALU.max, ALU.subtract).then_inc(hidl_sb, 1)

            def x3(i):
                at(dve, out_ps, i + 1)
                tt(x3T[:, :], pB0[:, :], x2T[:, :], ALU.add).then_inc(x3_sb, 1)
                at(dve, x3_sb, 2 * i + 1)
                dve.tensor_copy(x3p[0][:, :], x3T[:, :]).then_inc(x3_sb, 1)
                at(dve, x3_sb, 2 * i + 2)
                tt(x3p[1][:, :], x3T[:, :], x3p[0][:, :], ALU.subtract).then_inc(x3l_sb, 1)

            def result(i):
                at(dve, fin_ps, i + 2)
                at(dve, x3n_sb, i + 1)
                at(dve, st_out, 16 * (i + 1))
                tt(o_s[:, :, :].rearrange("p g d -> p (g d)"), pB2[:, :], x3n[:, :], ALU.add).then_inc(res_sb, 1)

            prepare_pooling()
            prepare_hits()
            scorer_low(0)
            wrap(I_E2, B, E2)
            pool_weights(0, 0)
            prepare_counts()
            pool_weights(0, 1)
            wrap(I_E3, B, E3)
            prepare_ids()
            x1(0)
            prepare_strength()
            prepare_products()
            prepare_bias()
            keys(0)
            scorer_low(1)
            mask_tokens(G, TILES)
            score_max(0, 0)
            score_max(0, 1)
            turn(0, 0)
            count_tokens(G, TILES)
            score_max(0, 2)
            turn(0, 1)
            score_max(0, 3)
            turn(0, 2)
            normalise(0, 0)
            turn(0, 3)
            pool_weights(1, 0)
            normalise(0, 1)
            pool_weights(1, 1)
            x2(0)
            x1(1)
            x2_low(0)

            def step_of(n, last, next_block=True):
                if last is not None:
                    x2_low(n - 1)
                mask_low(n - 1)
                keys(n)
                if next_block:
                    scorer_low(n + 1)
                    pool_weights(n + 1, 0)
                if last is None:
                    dve.wait_ge(bias_sb, 3)
                score_max(n, 0)
                score_max(n, 1)
                if last is not None:
                    result(last)
                if next_block:
                    pool_weights(n + 1, 1)
                turn(n, 0)
                score_max(n, 2)
                relu_low(n - 1, 0)
                turn(n, 1)
                score_max(n, 3)
                turn(n, 2)
                normalise(n, 0)
                relu_low(n - 1, 1)
                relu_low(n - 1, 2)
                relu_low(n - 1, 3)
                turn(n, 3)
                mask_low2(n - 1)
                normalise(n, 1)
                x3(n - 1)
                x2(n)
                if next_block:
                    x1(n + 1)

            step_of(1, None)
            with dve.Fori(2, NBLK - 1) as n:
                step_of(n, n - 2)
            step_of(NBLK - 1, NBLK - 3, False)
            x2_low(NBLK - 1)
            mask_low(NBLK - 1)
            result(NBLK - 2)
            for c in range(FC):
                relu_low(NBLK - 1, c)
            mask_low2(NBLK - 1)
            x3(NBLK - 1)
            result(NBLK - 1)


P_COUNT = 20
P_E3 = 25
P_PRODUCTS = 33
P_BIAS = 39
L0_STEPS = 14


def kernel(**inputs):
    import numpy as np
    import concourse.bacc as bacc
    from concourse.bass_utils import run_bass_kernel_spmd

    a = {k: np.asarray(v) for k, v in inputs.items()}

    def ca(x):
        return np.ascontiguousarray(x)

    def quads(x):
        return np.tile(x, (Q4, 1))

    def by_tile(x):
        return np.repeat(x.reshape(TILES, Q4).T, S, axis=0)

    x = a["x"]
    ints = np.zeros((P, I_END), np.int32)
    ints[:, I_TYPE:I_E2] = by_tile(a["itok_B_0_2"])
    ints[:, I_E2:I_E3] = a["itok_B_0_7"][None, :]
    ints[:, I_E3:I_IDX] = a["itok_B_0_15"][None, :]
    ints[E3, I_E3:I_IDX] = E3 - 1
    ints[:, I_IDX:I_END] = quads(a["itok_Sx32_0_1023"])
    bools = quads(np.concatenate([a["mask_SxS_bk0"], a["mask_Sx32_bk1"]], axis=1)).view(np.int32)
    p = np.arange(P)
    cols = np.zeros((P, C_END), np.float32)
    cols[:, C_SIGN:C_SIGN + S] = np.sign((p % S)[:, None] - np.arange(S)[None, :])
    cols[:, C_IOTA:C_IOTA + S] = np.arange(S)[None, :]
    cols[:, C_U:C_U + TILES] = by_tile(a["condB_uprev"])
    cols[:, C_HEAD:C_HEAD + H4] = ((p % S) // DH)[:, None] == np.arange(H4)[None, :]
    cols[:, C_BQ:C_BQ + HG] = quads(a["L1_cond_bq"].reshape(HG, S).T)
    cols[:, C_BK:C_BK + HG] = quads(a["L1_cond_bk"].reshape(HG, S).T)
    cols[:, C_FC1B:C_FC1B + FC] = a["L3_cond_fc1_b"].reshape(FC, P).T
    cols[:, C_E2] = p // (P // E2)
    cols[:, C_E3] = np.minimum(p, E3 - 1)
    cols[:, C_BO] = a["L1_cond_bo"]
    by_head = lambda w: w.reshape(HG, H4, DH, -1).transpose(1, 0, 2, 3).reshape(D, -1)
    cols[:, C_BV] = by_head(a["L1_cond_bv"])[:, 0]
    cols[0:TH * A0, C_B1] = np.tile(a["L0_cond_b1"], TH)
    cols[0:TH * A0, C_V:C_V + P] = np.tile(a["L0_cond_v"][:, None], (TH, P))
    cols[:, C_IDENT:C_END] = np.eye(P)
    attn_w = np.concatenate([np.tile(a["L0_cond_W1"], (1, TH)), a["L1_cond_Wq"].T, a["L1_cond_Wk"].T,
                             a["L1_cond_Wv"].T, by_head(a["L1_cond_Wo"].T)], axis=1)
    rank_w = np.zeros((E3 + 1, R_END), np.float32)
    rank_w[0:RANK, 0:R_FB] = np.concatenate([a["L2_cond_common_wi_a"], a["L2_cond_common_wi_b"].T,
                                             a["L2_cond_common_wo_a"], a["L2_cond_common_wo_b"].T], axis=1)
    rank_w[0:E3, R_FB + SHARED:R_END] = a["L3_cond_experts_b"]
    rank_w[E3, R_FB:R_FB + SHARED] = a["L3_cond_fc2_b"]
    chunks = lambda w: w.T.reshape(FC, P, -1).transpose(1, 0, 2)

    flat = lambda w: chunks(w).reshape(P, -1)
    ffn_w = np.concatenate([
        a["L2_cond_experts_wi_a"].reshape(P, D).T,
        a["L2_cond_experts_wi_b"].transpose(0, 2, 1).reshape(P, F),
        a["L2_cond_experts_wo_b"].transpose(0, 2, 1).reshape(P, D),
        a["L3_cond_fc1_w"].T,
        flat(a["L2_cond_experts_wo_a"].reshape(P, F)),
        a["L2_cond_wi"].T,
        flat(a["L2_cond_wo"])], axis=1)

    arrays = {
        "xt": x.reshape(NBLK, TOK, D).transpose(0, 2, 1),
        "xn": x.reshape(NBLK, G, P, D).transpose(0, 2, 1, 3),
        "ints": ints, "bools": bools, "cols": cols, "attn_w": attn_w, "rank_w": rank_w, "ffn_w": ffn_w,
        "fc2t": chunks(a["L3_cond_fc2_w"]),
        "e3t": a["L3_cond_experts_w"].reshape(E3, PART, FC, P).transpose(3, 0, 2, 1),
    }
    nc = bacc.Bacc("TRN2", target_bir_lowering=False, num_devices=1)
    args = {}
    for name in arrays:
        arrays[name] = ca(arrays[name])
        args[name] = nc.dram_tensor(name + "_dram", arrays[name].shape, mybir.dt.from_np(arrays[name].dtype),
                                    kind="ExternalInput").ap()
    out = nc.dram_tensor("out_dram", (NBLK, P, G, D), F32, kind="ExternalOutput").ap()
    cond_resid_kernel(nc, out=out, **args)
    r = run_bass_kernel_spmd(nc, [{k + "_dram": v for k, v in arrays.items()}], core_ids=[0])
    got = r.results[0]["out_dram"]
    return np.ascontiguousarray(got.transpose(0, 2, 1, 3)).reshape(B, S, D)
```
